# Optimizing a Trainium2 kernel written in Bass

```python
import numpy as np
import jax
import jax.numpy as jnp

def _softmax(x, axis=-1):
    return jax.nn.softmax(x, axis=axis)

def _gelu(x):
    return jax.nn.gelu(x, approximate=True)

def _silu(x):
    return jax.nn.silu(x)

def _sigmoid(x):
    return jax.nn.sigmoid(x)

def _layernorm(x, axis=-1, eps=1e-05):
    m = jnp.mean(x, axis=axis, keepdims=True)
    v = jnp.var(x, axis=axis, keepdims=True)
    return (x - m) / jnp.sqrt(v + eps)

def _scatter_add(tgt, idx, src, axis=0):
    return tgt.at[idx].add(src)

def _segment_sum(src, seg, n):
    return jax.ops.segment_sum(src, seg, n)
kernel_name = 'mk_adaln_ffn_d2_seqx_r8_2ab7d7'

def setup_inputs(seed: int=0):
    np.random.seed(seed)
    _w = jnp.asarray

    def _rec_inputs():
        import jax
        import jax.numpy as jnp
        _rk = jax.random.key(seed)
        x = -5.074e-05 + 0.9999 * jax.random.normal(jax.random.fold_in(_rk, 1), (8, 256, 128), jnp.float32)
        _lenS = 256 - jax.random.randint(jax.random.fold_in(_rk, 7), (8,), 0, max(1, 256 // 4) + 1, jnp.int32)
        _lenS2 = 256 - jax.random.randint(jax.random.fold_in(_rk, 8), (8,), 0, max(1, 256 // 4) + 1, jnp.int32)
        cond_1024 = jax.random.uniform(jax.random.fold_in(_rk, 11), (8, 128), jnp.float32, 0.0, 0.999973)
        return (x, cond_1024)
    x, cond_1024 = _rec_inputs()

    def _L0_cond_setup():
        import jax, jax.numpy as jnp
        import numpy as np
        from jax import lax
        ALPHA_LO = float(np.exp(-1.0 / 5.0))
        ALPHA_HI = float(np.exp(-1.0 / 25.0))
        THRESHOLD = 1.0

        @jax.custom_vjp
        def spike_boxcar(x):
            return (x > 0).astype(x.dtype)

        def _spike_fwd(x):
            return (spike_boxcar(x), x)

        def _spike_bwd(x, g):
            mask = ((x > -0.5) & (x <= 0.5)).astype(g.dtype)
            return (g * mask,)
        spike_boxcar.defvjp(_spike_fwd, _spike_bwd)
        key = jax.random.key(seed)
        kx, kW, kV, ka, ku, ks = jax.random.split(key, 6)
        B, T, I, H = (64, 125, 128, 128)
        x = jax.random.normal(kx, (B, T, I), dtype=jnp.float32)
        W = jax.random.normal(kW, (H, I), dtype=jnp.float32) / np.sqrt(I)
        V = jnp.linalg.qr(jax.random.normal(kV, (H, H), dtype=jnp.float32))[0]
        alpha = jax.random.uniform(ka, (H,), dtype=jnp.float32, minval=ALPHA_LO, maxval=ALPHA_HI)
        ut0 = jax.random.uniform(ku, (B, H), dtype=jnp.float32)
        st0 = jax.random.uniform(ks, (B, H), dtype=jnp.float32)
        return {'x': x, 'W': W, 'V': V, 'alpha': alpha, 'ut0': ut0, 'st0': st0}
    _L0_cond_all = _L0_cond_setup()
    _L0_cond_in = {k: v for k, v in _L0_cond_all.items() if k in ('W', 'V', 'alpha')}
    del _L0_cond_all

    def _L0_ffn_setup():
        import jax, jax.numpy as jnp
        import numpy as np
        NUM_EXPERTS = 8
        TOP_K = 2
        key = jax.random.key(seed)
        ks = jax.random.split(key, 6)
        B, S, D, H, E = (4, 128, 128, 256, NUM_EXPERTS)
        x = jax.random.normal(ks[0], (B, S, D), dtype=jnp.float32)
        Wg = jax.random.normal(ks[1], (D, E), dtype=jnp.float32) * 0.02
        W1 = jax.random.normal(ks[2], (E, D, H), dtype=jnp.float32) * 0.02
        b1 = jax.random.normal(ks[3], (E, H), dtype=jnp.float32) * 0.02
        W2 = jax.random.normal(ks[4], (E, H, D), dtype=jnp.float32) * 0.02
        b2 = jax.random.normal(ks[5], (E, D), dtype=jnp.float32) * 0.02
        return {'x': x, 'Wg': Wg, 'W1': W1, 'b1': b1, 'W2': W2, 'b2': b2}
    _L0_ffn_all = _L0_ffn_setup()
    _L0_ffn_in = {k: v for k, v in _L0_ffn_all.items() if k in ('Wg', 'W1', 'b1', 'W2', 'b2')}
    del _L0_ffn_all

    def _L1_cond_setup():
        import jax, jax.numpy as jnp
        import numpy as np
        N, T, D, H = (64, 64, 128, 128)

        def lstm_scan(x, h0, Wx, Wh, b):
            xW = jnp.einsum('ntd,dg->ntg', x, Wx) + b
            Hdim = h0.shape[1]
            c0 = jnp.zeros_like(h0)

            def step(carry, xw_t):
                prev_h, prev_c = carry
                a = xw_t + prev_h @ Wh
                i = jax.nn.sigmoid(a[:, :Hdim])
                f = jax.nn.sigmoid(a[:, Hdim:2 * Hdim])
                o = jax.nn.sigmoid(a[:, 2 * Hdim:3 * Hdim])
                g = jnp.tanh(a[:, 3 * Hdim:])
                next_c = f * prev_c + i * g
                next_h = o * jnp.tanh(next_c)
                return ((next_h, next_c), next_h)
            _, hs = jax.lax.scan(step, (h0, c0), jnp.swapaxes(xW, 0, 1))
            return jnp.swapaxes(hs, 0, 1)
        key = jax.random.key(seed)
        k1, k2, k3, k4 = jax.random.split(key, 4)
        x = jax.random.normal(k1, (N, T, D), dtype=jnp.float32)
        h0 = jax.random.normal(k2, (N, H), dtype=jnp.float32)
        Wx = jax.random.normal(k3, (D, 4 * H), dtype=jnp.float32) / np.sqrt(D)
        Wh = jax.random.normal(k4, (H, 4 * H), dtype=jnp.float32) / np.sqrt(H)
        b = jnp.zeros((4 * H,), dtype=jnp.float32)
        return {'x': x, 'h0': h0, 'Wx': Wx, 'Wh': Wh, 'b': b}
    _L1_cond_all = _L1_cond_setup()
    _L1_cond_in = {k: v for k, v in _L1_cond_all.items() if k in ('Wx', 'Wh', 'b')}
    del _L1_cond_all

    def _L1_ffn_setup():
        import jax, jax.numpy as jnp
        import numpy as np
        DIM = 128
        DEPTH = 6
        HEADS = 16
        DIM_HEAD = 64
        WINDOW = 32
        INNER = HEADS * DIM_HEAD
        DIM_INNER = int(DIM * 4 * 2 / 3)
        QK_SCALE = 8.0

        def shift_tokens(t):
            a, s = jnp.split(t, 2, -1)
            s = jnp.pad(s, ((0, 0), (1, 0), (0, 0)))[:, :-1]
            return jnp.concatenate([a, s], -1)

        def l2norm(t):
            return t / jnp.maximum(jnp.linalg.norm(t, axis=-1, keepdims=True), 1e-12)

        def rotate_half(x):
            x1, x2 = jnp.split(x, 2, -1)
            return jnp.concatenate([-x2, x1], -1)

        def rotary_tables(n):
            half = jnp.arange(0, DIM_HEAD, 2, dtype=jnp.float32)
            inv_freq = 1.0 / 10000.0 ** (half / DIM_HEAD)
            t = jnp.arange(n, dtype=jnp.float32)
            freqs = t[:, None] * inv_freq[None, :]
            freqs = jnp.concatenate([freqs, freqs], -1)
            base_scale = (half + 0.4 * DIM_HEAD) / (1.4 * DIM_HEAD)
            power = (t - n // 2) / (WINDOW // 2)
            scale = base_scale[None, :] ** power[:, None]
            scale = jnp.concatenate([scale, scale], -1)
            return (freqs, scale)

        def local_attention(q, k, v):
            b, h, n, d = q.shape
            w = WINDOW
            nw = n // w
            bq = q.reshape(b, h, nw, w, d)
            bk = k.reshape(b, h, nw, w, d)
            bv = v.reshape(b, h, nw, w, d)

            def look(t):
                p = jnp.pad(t, ((0, 0), (0, 0), (1, 0), (0, 0), (0, 0)))
                return jnp.concatenate([p[:, :, :nw], p[:, :, 1:]], axis=3)
            bk2, bv2 = (look(bk), look(bv))
            seq = jnp.arange(n).reshape(nw, w)
            seq_p = jnp.pad(seq, ((1, 0), (0, 0)), constant_values=-1)
            jt = jnp.concatenate([seq_p[:nw], seq_p[1:]], axis=1)
            it = seq[:, :, None]
            jb = jt[:, None, :]
            mask = (it < jb) | (it > jb + w) | (jb == -1)
            sim = jnp.einsum('bhwie,bhwje->bhwij', bq, bk2) * QK_SCALE
            sim = jnp.where(mask, -jnp.finfo(sim.dtype).max, sim)
            attn = jax.nn.softmax(sim, -1)
            out = jnp.einsum('bhwij,bhwje->bhwie', attn, bv2)
            return out.reshape(b, h, n, d)

        def attn_layer(x, Wqkv, qs, ksc, Wo):
            b, n, _ = x.shape
            qkv = x @ Wqkv
            q, k, v = jnp.split(qkv, 3, -1)
            sh = lambda t: t.reshape(b, n, HEADS, DIM_HEAD).transpose(0, 2, 1, 3)
            q, k, v = (sh(q), sh(k), sh(v))
            q = l2norm(q) * qs
            k = l2norm(k) * ksc
            freqs, scale = rotary_tables(n)
            cos, sin = (jnp.cos(freqs), jnp.sin(freqs))
            q = q * cos * scale + rotate_half(q) * sin * scale
            inv = 1.0 / scale
            k = k * cos * inv + rotate_half(k) * sin * inv
            out = local_attention(q, k, v)
            out = out.transpose(0, 2, 1, 3).reshape(b, n, INNER)
            return out @ Wo

        def ffn_layer(x, g, bln, W1, b1, W2, b2):
            mu = x.mean(-1, keepdims=True)
            var = ((x - mu) ** 2).mean(-1, keepdims=True)
            xn = (x - mu) / jnp.sqrt(var + 1e-05) * g + bln
            hg = xn @ W1 + b1
            a, gate = jnp.split(hg, 2, -1)
            return a * jax.nn.gelu(gate, approximate=False) @ W2 + b2
        key = jax.random.key(seed)
        ks = jax.random.split(key, 8)
        B, N = (2, 256)
        init = lambda k, shape: jax.random.normal(k, shape, jnp.float32) * 0.02
        return {'x': jax.random.normal(ks[0], (B, N, DIM), jnp.float32), 'Wqkv': init(ks[1], (DEPTH, DIM, 3 * INNER)), 'q_scale': jnp.ones((DEPTH, DIM_HEAD), jnp.float32), 'k_scale': jnp.ones((DEPTH, DIM_HEAD), jnp.float32), 'Wo': init(ks[2], (DEPTH, INNER, DIM)), 'ln_g': jnp.ones((DEPTH, DIM), jnp.float32), 'ln_b': jnp.zeros((DEPTH, DIM), jnp.float32), 'W1': init(ks[3], (DEPTH, DIM, 2 * DIM_INNER)), 'b1': jnp.zeros((DEPTH, 2 * DIM_INNER), jnp.float32), 'W2': init(ks[4], (DEPTH, DIM_INNER, DIM)), 'b2': jnp.zeros((DEPTH, DIM), jnp.float32)}
    _L1_ffn_all = _L1_ffn_setup()
    _L1_ffn_in = {k: v for k, v in _L1_ffn_all.items() if k in ('Wqkv', 'q_scale', 'k_scale', 'Wo', 'ln_g', 'ln_b', 'W1', 'b1', 'W2', 'b2')}
    del _L1_ffn_all
    return {'x': x, 'cond_1024': cond_1024, 'L0_cond_W': _L0_cond_in['W'], 'L0_cond_V': _L0_cond_in['V'], 'L0_cond_alpha': _L0_cond_in['alpha'], 'L0_ffn_Wg': _L0_ffn_in['Wg'], 'L0_ffn_W1': _L0_ffn_in['W1'], 'L0_ffn_b1': _L0_ffn_in['b1'], 'L0_ffn_W2': _L0_ffn_in['W2'], 'L0_ffn_b2': _L0_ffn_in['b2'], 'L1_cond_Wx': _L1_cond_in['Wx'], 'L1_cond_Wh': _L1_cond_in['Wh'], 'L1_cond_b': _L1_cond_in['b'], 'L1_ffn_Wqkv': _L1_ffn_in['Wqkv'], 'L1_ffn_q_scale': _L1_ffn_in['q_scale'], 'L1_ffn_k_scale': _L1_ffn_in['k_scale'], 'L1_ffn_Wo': _L1_ffn_in['Wo'], 'L1_ffn_ln_g': _L1_ffn_in['ln_g'], 'L1_ffn_ln_b': _L1_ffn_in['ln_b'], 'L1_ffn_W1': _L1_ffn_in['W1'], 'L1_ffn_b1': _L1_ffn_in['b1'], 'L1_ffn_W2': _L1_ffn_in['W2'], 'L1_ffn_b2': _L1_ffn_in['b2']}

def reference(x, cond_1024, L0_cond_W, L0_cond_V, L0_cond_alpha, L0_ffn_Wg, L0_ffn_W1, L0_ffn_b1, L0_ffn_W2, L0_ffn_b2, L1_cond_Wx, L1_cond_Wh, L1_cond_b, L1_ffn_Wqkv, L1_ffn_q_scale, L1_ffn_k_scale, L1_ffn_Wo, L1_ffn_ln_g, L1_ffn_ln_b, L1_ffn_W1, L1_ffn_b1, L1_ffn_W2, L1_ffn_b2):
    import jax
    import jax.numpy as jnp

    def _L0_cond_ref(x, W, V, alpha, ut0, st0):
        import jax, jax.numpy as jnp
        import numpy as np
        from jax import lax
        ALPHA_LO = float(np.exp(-1.0 / 5.0))
        ALPHA_HI = float(np.exp(-1.0 / 25.0))
        THRESHOLD = 1.0

        @jax.custom_vjp
        def spike_boxcar(x):
            return (x > 0).astype(x.dtype)

        def _spike_fwd(x):
            return (spike_boxcar(x), x)

        def _spike_bwd(x, g):
            mask = ((x > -0.5) & (x <= 0.5)).astype(g.dtype)
            return (g * mask,)
        spike_boxcar.defvjp(_spike_fwd, _spike_bwd)
        Wx = jnp.einsum('bti,hi->bth', x, W)
        a = jnp.clip(alpha, ALPHA_LO, ALPHA_HI)
        H = V.shape[0]
        Vz = V * (1.0 - jnp.eye(H, dtype=V.dtype))

        def step(carry, wx_t):
            ut, st = carry
            ut = a * (ut - st) + (1.0 - a) * (wx_t + st @ Vz)
            st = spike_boxcar(ut - THRESHOLD)
            return ((ut, st), st)
        Wx_t = jnp.swapaxes(Wx, 0, 1)
        _, s = lax.scan(step, (ut0, st0), Wx_t)
        return jnp.swapaxes(s, 0, 1)

    def _L0_ffn_ref(x, Wg, W1, b1, W2, b2):
        import jax, jax.numpy as jnp
        import numpy as np
        NUM_EXPERTS = 8
        TOP_K = 2
        B, S, D = x.shape
        E, _, H = W1.shape
        OUT = W2.shape[2]
        xm = x.reshape(-1, D)
        logits = xm @ Wg
        probs = jax.nn.softmax(logits, axis=-1)
        topk_p, topk_i = jax.lax.top_k(probs, TOP_K)
        flat_e = topk_i.reshape(-1)
        flat_p = topk_p.reshape(-1)
        order = jnp.argsort(flat_e)
        tok_idx = order // TOP_K
        e_sorted = flat_e[order]
        p_sorted = flat_p[order]
        xs = xm[tok_idx]
        y = jnp.zeros((xs.shape[0], OUT), dtype=xs.dtype)
        for e in range(E):
            h = jax.nn.relu(xs @ W1[e] + b1[e])
            ye = h @ W2[e] + b2[e]
            m = (e_sorted == e)[:, None].astype(xs.dtype)
            y = y + m * ye
        y = y * p_sorted[:, None]
        out = jnp.zeros((B * S, OUT), dtype=y.dtype).at[tok_idx].add(y)
        return out.reshape(B, S, OUT)

    def _L1_cond_ref(x, h0, Wx, Wh, b):
        import jax, jax.numpy as jnp
        import numpy as np
        N, T, D, H = (64, 64, 128, 128)

        def lstm_scan(x, h0, Wx, Wh, b):
            xW = jnp.einsum('ntd,dg->ntg', x, Wx) + b
            Hdim = h0.shape[1]
            c0 = jnp.zeros_like(h0)

            def step(carry, xw_t):
                prev_h, prev_c = carry
                a = xw_t + prev_h @ Wh
                i = jax.nn.sigmoid(a[:, :Hdim])
                f = jax.nn.sigmoid(a[:, Hdim:2 * Hdim])
                o = jax.nn.sigmoid(a[:, 2 * Hdim:3 * Hdim])
                g = jnp.tanh(a[:, 3 * Hdim:])
                next_c = f * prev_c + i * g
                next_h = o * jnp.tanh(next_c)
                return ((next_h, next_c), next_h)
            _, hs = jax.lax.scan(step, (h0, c0), jnp.swapaxes(xW, 0, 1))
            return jnp.swapaxes(hs, 0, 1)
        return lstm_scan(x, h0, Wx, Wh, b)

    def _L1_ffn_ref(x, Wqkv, q_scale, k_scale, Wo, ln_g, ln_b, W1, b1, W2, b2):
        import jax, jax.numpy as jnp
        import numpy as np
        DIM = 128
        DEPTH = 6
        HEADS = 16
        DIM_HEAD = 64
        WINDOW = 32
        INNER = HEADS * DIM_HEAD
        DIM_INNER = int(DIM * 4 * 2 / 3)
        QK_SCALE = 8.0

        def shift_tokens(t):
            a, s = jnp.split(t, 2, -1)
            s = jnp.pad(s, ((0, 0), (1, 0), (0, 0)))[:, :-1]
            return jnp.concatenate([a, s], -1)

        def l2norm(t):
            return t / jnp.maximum(jnp.linalg.norm(t, axis=-1, keepdims=True), 1e-12)

        def rotate_half(x):
            x1, x2 = jnp.split(x, 2, -1)
            return jnp.concatenate([-x2, x1], -1)

        def rotary_tables(n):
            half = jnp.arange(0, DIM_HEAD, 2, dtype=jnp.float32)
            inv_freq = 1.0 / 10000.0 ** (half / DIM_HEAD)
            t = jnp.arange(n, dtype=jnp.float32)
            freqs = t[:, None] * inv_freq[None, :]
            freqs = jnp.concatenate([freqs, freqs], -1)
            base_scale = (half + 0.4 * DIM_HEAD) / (1.4 * DIM_HEAD)
            power = (t - n // 2) / (WINDOW // 2)
            scale = base_scale[None, :] ** power[:, None]
            scale = jnp.concatenate([scale, scale], -1)
            return (freqs, scale)

        def local_attention(q, k, v):
            b, h, n, d = q.shape
            w = WINDOW
            nw = n // w
            bq = q.reshape(b, h, nw, w, d)
            bk = k.reshape(b, h, nw, w, d)
            bv = v.reshape(b, h, nw, w, d)

            def look(t):
                p = jnp.pad(t, ((0, 0), (0, 0), (1, 0), (0, 0), (0, 0)))
                return jnp.concatenate([p[:, :, :nw], p[:, :, 1:]], axis=3)
            bk2, bv2 = (look(bk), look(bv))
            seq = jnp.arange(n).reshape(nw, w)
            seq_p = jnp.pad(seq, ((1, 0), (0, 0)), constant_values=-1)
            jt = jnp.concatenate([seq_p[:nw], seq_p[1:]], axis=1)
            it = seq[:, :, None]
            jb = jt[:, None, :]
            mask = (it < jb) | (it > jb + w) | (jb == -1)
            sim = jnp.einsum('bhwie,bhwje->bhwij', bq, bk2) * QK_SCALE
            sim = jnp.where(mask, -jnp.finfo(sim.dtype).max, sim)
            attn = jax.nn.softmax(sim, -1)
            out = jnp.einsum('bhwij,bhwje->bhwie', attn, bv2)
            return out.reshape(b, h, n, d)

        def attn_layer(x, Wqkv, qs, ksc, Wo):
            b, n, _ = x.shape
            qkv = x @ Wqkv
            q, k, v = jnp.split(qkv, 3, -1)
            sh = lambda t: t.reshape(b, n, HEADS, DIM_HEAD).transpose(0, 2, 1, 3)
            q, k, v = (sh(q), sh(k), sh(v))
            q = l2norm(q) * qs
            k = l2norm(k) * ksc
            freqs, scale = rotary_tables(n)
            cos, sin = (jnp.cos(freqs), jnp.sin(freqs))
            q = q * cos * scale + rotate_half(q) * sin * scale
            inv = 1.0 / scale
            k = k * cos * inv + rotate_half(k) * sin * inv
            out = local_attention(q, k, v)
            out = out.transpose(0, 2, 1, 3).reshape(b, n, INNER)
            return out @ Wo

        def ffn_layer(x, g, bln, W1, b1, W2, b2):
            mu = x.mean(-1, keepdims=True)
            var = ((x - mu) ** 2).mean(-1, keepdims=True)
            xn = (x - mu) / jnp.sqrt(var + 1e-05) * g + bln
            hg = xn @ W1 + b1
            a, gate = jnp.split(hg, 2, -1)
            return a * jax.nn.gelu(gate, approximate=False) @ W2 + b2
        for i in range(DEPTH):
            x = attn_layer(shift_tokens(x), Wqkv[i], q_scale[i], k_scale[i], Wo[i]) + x
            x = ffn_layer(shift_tokens(x), ln_g[i], ln_b[i], W1[i], b1[i], W2[i], b2[i]) + x
        return x
    x = x + _L0_ffn_ref(_L0_cond_ref(x, L0_cond_W, L0_cond_V, L0_cond_alpha, cond_1024, cond_1024), L0_ffn_Wg, L0_ffn_W1, L0_ffn_b1, L0_ffn_W2, L0_ffn_b2)
    x = x + _L1_ffn_ref(_L1_cond_ref(x, cond_1024, L1_cond_Wx, L1_cond_Wh, L1_cond_b), L1_ffn_Wqkv, L1_ffn_q_scale, L1_ffn_k_scale, L1_ffn_Wo, L1_ffn_ln_g, L1_ffn_ln_b, L1_ffn_W1, L1_ffn_b1, L1_ffn_W2, L1_ffn_b2)
    return x

_drawn_inputs = setup_inputs


def setup_inputs(seed=0):
    import zlib

    import numpy as np

    out = dict(_drawn_inputs(seed))
    spreads = {'L1_cond_b': (0.0, 0.1),
     'L1_ffn_q_scale': (1.0, 0.6),
     'L1_ffn_k_scale': (1.0, 0.6),
     'L1_ffn_ln_g': (1.0, 0.6),
     'L1_ffn_ln_b': (0.0, 0.8),
     'L1_ffn_b1': (0.0, 0.51),
     'L1_ffn_b2': (0.0, 0.1)}
    factors = {'cond_1024': 8.0,
     'L0_cond_W': 8.0,
     'L0_cond_V': 8.0,
     'L0_cond_alpha': 8.0,
     'L0_ffn_Wg': 8.0,
     'L0_ffn_W1': 8.0,
     'L0_ffn_b1': 8.0,
     'L0_ffn_W2': 8.0,
     'L0_ffn_b2': 8.0}
    for name, (base, spread) in spreads.items():
        noise = np.random.default_rng([zlib.crc32(name.encode()), seed]).standard_normal(out[name].shape)
        drawn = base * np.exp(spread * noise) if base else spread * noise
        out[name] = jnp.asarray(drawn.astype(out[name].dtype))
    for name, factor in factors.items():
        out[name] = (out[name] * factor).astype(out[name].dtype)
    return out
```

```python
import numpy as np
from contextlib import ExitStack
import concourse.bass as bass
from concourse import mybir

F32 = mybir.dt.float32
BF16 = mybir.dt.bfloat16
U32 = mybir.dt.uint32
ALU = mybir.AluOpType
ACT = mybir.ActivationFunctionType
AX = mybir.AxisListType

B, T, D = 8, 256, 128
TOK = B * T
E, EH = 8, 256
CH = 512
NCH = TOK // CH
STEPS_CH = CH // B
HALVES = EH // 128
LAYERS, HEADS, HD, WIN = 6, 16, 64, 32
GROUPS, GH = 4, 4
QK = 2 * GH * HD
VC = GH * HD
GC = QK + VC
TILES = T // 128
FI = 341
FCH, FW = 3, 114
ALPHA_LO, ALPHA_HI = float(np.exp(-1.0 / 5.0)), float(np.exp(-1.0 / 25.0))
RS = 256.0
UNR = 8


def spiking_and_experts(nc, io, x1, lstm_xw):
    ctx = ExitStack()
    with ctx:
        def sb(name, shape, dt=F32):
            return ctx.enter_context(nc.sbuf_tensor(name, shape, dt))

        def pb(name, shape, dt=F32):
            return ctx.enter_context(nc.psum_tensor(name, shape, dt))

        def sem(name):
            return ctx.enter_context(nc.semaphore(name))

        xT = sb("xT", [128, TOK])
        condT = sb("condT", [128, B])
        wlif = sb("wlif", [128, 128])
        vlif = sb("vlif", [128, 128])
        al_col = sb("al_col", [128, 1])
        al_row = sb("al_row", [128, 128])
        ident = sb("ident", [128, 128])
        off_diag = sb("off_diag", [128, 128])
        iota = sb("iota", [128, E])
        wg = sb("wg", [128, E])
        w1 = sb("w1", [128, E * EH])
        b1 = sb("b1", [128, E * HALVES])
        w2 = sb("w2", [128, E * HALVES * 128])
        b2 = sb("b2", [E, 128])
        wx = sb("wx", [128, 4 * 128])
        bx = sb("bx", [128, 4])

        oma = sb("oma", [128, 1])
        noma = sb("noma", [128, 1])
        keep = sb("keep", [128, 128])
        vmat = sb("vmat", [128, 128])
        diag = sb("diag", [128, 128])
        vparts = sb("vparts", [128, 3, 128], BF16)
        vrest = sb("vrest", [128, 128])
        drive = sb("drive", [128, TOK])
        spikes = sb("spikes", [128, TOK], BF16)
        gap = sb("gap", [128, B])
        thr = sb("thr", [128, B])
        w1p = sb("w1p", [128, 3, E * EH], BF16)
        w1r = sb("w1r", [128, E * EH])
        wgp = sb("wgp", [128, 3, E], BF16)
        wgr = sb("wgr", [128, E])

        chunk = sb("chunk", [128, CH], BF16)
        lmax = sb("lmax", [128, 4])
        lsub = sb("lsub", [128, 4, E])
        lexp = sb("lexp", [128, 4, E])
        lsum = sb("lsum", [128, 4])
        spare = sb("spare", [128, 1])
        probs = sb("probs", [128, 4, E])
        top = sb("top", [128, 4, 8])
        topi = sb("topi", [128, 4, 8], U32)
        topf = sb("topf", [128, 4, 8])
        pick = sb("pick", [128, 2, 4, E])
        gate = sb("gate", [128, 4, E])
        gateT = sb("gateT", [E, 4, 128])
        hid = sb("hid", [128, 2, HALVES, CH])
        acc = sb("acc", [128, 4, 128])
        x1c = sb("x1c", [128, CH])

        p_rec = [pb(f"p_rec{i}", [128, 512]) for i in range(2)]
        p_h = [pb(f"p_h{i}", [128, CH]) for i in range(2)]
        p_y = [pb(f"p_y{i}", [128, CH]) for i in range(2)]
        p_g = pb("p_g", [128, 512])
        p_t = pb("p_t", [128, 512])

        in_lif, in_moe = sem("in_lif"), sem("in_moe")
        vready, wx_mm, drive_ok = sem("vready"), sem("wx_mm"), sem("drive_ok")
        prep, moe_prep = sem("prep"), sem("moe_prep")
        rec_mm, spike_ok, rec_ch = sem("rec_mm"), sem("spike_ok"), sem("rec_ch")
        chunk_ok, logit_mm, lsub_ok, lexp_ok, gch = (
            sem("chunk_ok"), sem("logit_mm"), sem("lsub_ok"), sem("lexp_ok"), sem("gch"))
        gate_ok, gateT_mm, gateT_ok = sem("gate_ok"), sem("gateT_mm"), sem("gateT_ok")
        h_mm, h_ok, y_mm, acc_ok = sem("h_mm"), sem("h_ok"), sem("y_mm"), sem("acc_ok")
        out_mm, x1_ok, xw_mm, xw_ok = sem("out_mm"), sem("x1_ok"), sem("xw_mm"), sem("xw_ok")

        block = ctx.enter_context(nc.Block())

        @block.sync
        def _(sp):
            for dst, name in ((al_col, "alpha_col"), (wlif, "wlif"), (vlif, "vlif"), (ident, "ident"),
                              (off_diag, "off_diag"), (condT, "condT"), (xT, "xT")):
                sp.dma_start(dst[:], io[name]).then_inc(in_lif, 16)
            sp.dma_start(al_row[:], io["alpha_row"].partition_broadcast(128)).then_inc(in_lif, 16)
            for dst, name in ((w1, "e_w1"), (wg, "wg"), (iota, "iota"), (b1, "e_b1"), (w2, "e_w2"),
                              (b2, "e_b2"), (wx, "wx"), (bx, "bx")):
                sp.dma_start(dst[:], io[name]).then_inc(in_moe, 16)

        @block.tensor
        def _(pe):
            pe.wait_ge(in_lif, 128)
            for c in range(NCH):
                if c >= 2:
                    pe.wait_ge(drive_ok, c - 1)
                pe.matmul(p_h[c % 2][:], wlif[:], xT[:, c * CH:(c + 1) * CH], start=True, stop=True).then_inc(wx_mm, 1)
            pe.wait_ge(vready, 1)
            pe.matmul(p_rec[0][:, 0:B], vmat[:], condT[:], start=True, stop=True).then_inc(rec_mm, 1)

            def step(t, bank, count):
                pe.wait_ge(spike_ok, count)
                for k in range(3):
                    last = pe.matmul(p_rec[bank][:, 0:B], vparts[:, k, :], spikes[:, bass.ds(t * B - B, B)],
                                     start=(k == 0), stop=(k == 2))
                last.then_inc(rec_mm, 1)

            for t in range(1, UNR):
                step(t, t % 2, t)
            with pe.Fori(1, T // UNR) as i:
                t0 = i * UNR
                for j in range(UNR):
                    step(t0 + j, j % 2, t0 + j)

            with pe.Fori(0, NCH) as c:
                pe.wait_ge(chunk_ok, c + 1)
                for j in range(4):
                    for k in range(3):
                        last = pe.matmul(p_g[:, j * E:(j + 1) * E], chunk[:, j * 128:(j + 1) * 128], wgp[:, k, :],
                                         start=(k == 0), stop=(k == 2))
                last.then_inc(logit_mm, 1)

                def up(e):
                    for h in range(HALVES):
                        n = e * HALVES + h
                        if n >= 2:
                            pe.wait_ge(h_ok, c * (E * HALVES) + n - 1)
                        for k in range(3):
                            last = pe.matmul(p_h[n % 2][:], w1p[:, k, e * EH + h * 128:e * EH + (h + 1) * 128],
                                             chunk[:], start=(k == 0), stop=(k == 2))
                        last.then_inc(h_mm, 1)

                def down(e):
                    pe.wait_ge(h_ok, c * (E * HALVES) + e * HALVES + HALVES)
                    if e >= 2:
                        pe.wait_ge(acc_ok, c * E + e - 1)
                    for j in range(4):
                        for h in range(HALVES):
                            last = pe.matmul(p_y[e % 2][:, j * 128:(j + 1) * 128], hid[:, e % 2, h, j * 128:(j + 1) * 128],
                                             w2[:, (e * HALVES + h) * 128:(e * HALVES + h + 1) * 128],
                                             start=(h == 0), stop=(h == HALVES - 1))
                    last.then_inc(y_mm, 1)

                up(0)
                for e in range(E):
                    if e + 1 < E:
                        up(e + 1)
                    down(e)
                pe.wait_ge(gate_ok, c + 1)
                for j in range(4):
                    last = pe.transpose(p_g[0:E, j * 128:(j + 1) * 128], gate[:, j, :], ident[:])
                last.then_inc(gateT_mm, 1)
                pe.wait_ge(acc_ok, c * E + E)
                pe.wait_ge(gateT_ok, c + 1)
                for j in range(4):
                    pe.matmul(p_t[:, j * 128:(j + 1) * 128], acc[:, j, :], ident[:], start=True, stop=False)
                    last = pe.matmul(p_t[:, j * 128:(j + 1) * 128], b2[:], gateT[:, j, :], start=False, stop=True)
                last.then_inc(out_mm, 1)
                pe.wait_ge(x1_ok, c + 1)
                for g in range(4):
                    if g >= 2:
                        pe.wait_ge(xw_ok, c * 4 + g - 1)
                    pe.matmul(p_h[g % 2][:], wx[:, g * 128:(g + 1) * 128], x1c[:], start=True, stop=True).then_inc(xw_mm, 1)
                pe.wait_ge(xw_ok, c * 4 + 4)

        @block.scalar
        def _(act):
            with act.Fori(0, NCH) as c:
                for n in range(E * HALVES):
                    act.wait_ge(h_mm, c * (E * HALVES) + n + 1)
                    e, h = divmod(n, HALVES)
                    if e >= 2:
                        act.wait_ge(y_mm, c * E + e - 1)
                    act.activation(hid[:, e % 2, h, :], p_h[n % 2][:], ACT.Relu, bias=b1[:, n:n + 1]).then_inc(h_ok, 1)
                    if n == 1:
                        act.wait_ge(lsub_ok, c + 1)
                        act.activation(lexp[:], lsub[:], ACT.Exp).then_inc(lexp_ok, 1)
                act.wait_ge(gateT_mm, c + 1)
                act.activation(gateT[:].rearrange("e j p -> e (j p)"), p_g[0:E, :], ACT.Copy).then_inc(gateT_ok, 1)
                for g in range(4):
                    act.wait_ge(xw_mm, c * 4 + g + 1)
                    dst = lstm_xw[:, bass.ds(c * (STEPS_CH * 4 * B), STEPS_CH * 4 * B)].rearrange(
                        "p (t g b) -> p t g b", g=4, b=B)[:, :, g, :]
                    act.activation(dst, p_h[g % 2][:].rearrange("p (t b) -> p t b", b=B), ACT.Identity,
                                   bias=bx[:, g:g + 1]).then_inc(xw_ok, 1)

        @block.vector
        def _(dve):
            done = [0]

            def link(ins):
                done[0] += 1
                ins.then_inc(prep, 1)
                dve.wait_ge(prep, done[0])

            dve.wait_ge(in_lif, 128)
            link(dve.tensor_scalar(al_col[:], al_col[:], ALPHA_LO, ALPHA_HI, ALU.max, ALU.min))
            dve.tensor_scalar(al_row[:], al_row[:], ALPHA_LO, ALPHA_HI, ALU.max, ALU.min)
            dve.tensor_scalar(oma[:], al_col[:], -1.0, 1.0, ALU.mult, ALU.add)
            link(dve.tensor_scalar(noma[:], al_col[:], 1.0, -1.0, ALU.mult, ALU.add))
            link(dve.tensor_scalar(keep[:], al_row[:], -1.0, 1.0, ALU.mult, ALU.add))
            link(dve.tensor_tensor(keep[:], keep[:], off_diag[:], ALU.mult))
            dve.tensor_tensor(vmat[:], vlif[:], keep[:], ALU.mult)
            link(dve.tensor_tensor(diag[:], al_row[:], ident[:], ALU.mult))
            link(dve.tensor_tensor(vmat[:], vmat[:], diag[:], ALU.subtract))
            dve.nop().then_inc(vready, 1)

            def split(parts, src, rest):
                link(dve.tensor_copy(parts(0), src))
                link(dve.tensor_tensor(rest, src, parts(0), ALU.subtract))
                link(dve.tensor_copy(parts(1), rest))
                link(dve.tensor_tensor(rest, rest, parts(1), ALU.subtract))
                link(dve.tensor_copy(parts(2), rest))

            split(lambda k: vparts[:, k, :], vmat[:], vrest[:])
            for c in range(NCH):
                dve.wait_ge(wx_mm, c + 1)
                ins = dve.tensor_scalar(drive[:, c * CH:(c + 1) * CH], p_h[c % 2][:], noma[:], oma[:], ALU.mult, ALU.add)
                ins.then_inc(drive_ok, 1)
            dve.wait_ge(drive_ok, NCH)
            link(dve.tensor_scalar(gap[:], condT[:], -1.0, 1.0, ALU.mult, ALU.add))
            dve.scalar_tensor_tensor(thr[:], gap[:], al_col[:], drive[:, 0:B], ALU.mult, ALU.add).then_inc(rec_ch, 1)

            def step(t, bank, count):
                dve.wait_ge(rec_ch, count)
                dve.wait_ge(rec_mm, t + 1)
                dve.tensor_tensor(spikes[:, bass.ds(t * B, B)], p_rec[bank][:, 0:B], thr[:], ALU.is_gt).then_inc(spike_ok, 1)
                dve.tensor_tensor(gap[:], thr[:], p_rec[bank][:, 0:B], ALU.subtract).then_inc(rec_ch, 1)
                dve.wait_ge(rec_ch, count + 1)
                dve.scalar_tensor_tensor(thr[:], gap[:], al_col[:], drive[:, bass.ds(t * B + B, B)],
                                         ALU.mult, ALU.add).then_inc(rec_ch, 1)

            with dve.Fori(0, T // UNR - 1) as i:
                t0 = i * UNR
                for j in range(UNR):
                    step(t0 + j, j % 2, 2 * t0 + 2 * j + 1)
            for t in range(T - UNR, T):
                if t < T - 1:
                    step(t, t % 2, 2 * t + 1)
            dve.wait_ge(rec_ch, 2 * T - 1)
            dve.wait_ge(rec_mm, T)
            dve.tensor_tensor(spikes[:, TOK - B:TOK], p_rec[(T - 1) % 2][:, 0:B], thr[:], ALU.is_gt).then_inc(spike_ok, 1)

            dve.wait_ge(in_moe, 128)
            split(lambda k: wgp[:, k, :], wg[:], wgr[:])
            split(lambda k: w1p[:, k, :], w1[:], w1r[:])
            dve.wait_ge(spike_ok, T)
            with dve.Fori(0, NCH) as c:
                dve.tensor_copy(chunk[:], spikes[:, bass.ds(c * CH, CH)]).then_inc(chunk_ok, 1)
                dve.wait_ge(logit_mm, c + 1)
                LINKS = 9
                k = [0]

                def link_c(ins):
                    k[0] += 1
                    ins.then_inc(gch, 1)
                    dve.wait_ge(gch, c * LINKS + k[0])

                lg = p_g[:, 0:4 * E].rearrange("p (j e) -> p j e", e=E)
                link_c(dve.tensor_reduce(lmax[:], lg, AX.X, ALU.max))
                dve.tensor_tensor(lsub[:], lg, lmax[:].unsqueeze(2).broadcast_to([128, 4, E]), ALU.subtract).then_inc(lsub_ok, 1)
                dve.wait_ge(lexp_ok, c + 1)
                link_c(dve.tensor_reduce(lsum[:], lexp[:], AX.X, ALU.add))
                link_c(dve.reciprocal(lsum[:], lsum[:]))
                link_c(dve.tensor_tensor(probs[:], lexp[:], lsum[:].unsqueeze(2).broadcast_to([128, 4, E]), ALU.mult))
                dve.tensor_copy(spare[:], lsum[:, 0:1])
                for j in range(4):
                    ins = dve.max(top[:, j, :], probs[:, j, :])
                link_c(ins)
                dve.tensor_copy(spare[:], lsum[:, 0:1])
                for j in range(4):
                    ins = dve.max_index(topi[:, j, :], top[:, j, :], probs[:, j, :])
                link_c(ins)
                link_c(dve.tensor_copy(topf[:], topi[:]))
                for j in range(4):
                    for r in range(2):
                        ins = dve.tensor_scalar(pick[:, r, j, :], iota[:], topf[:, j, r:r + 1], top[:, j, r:r + 1],
                                                ALU.is_equal, ALU.mult)
                link_c(ins)
                dve.tensor_tensor(gate[:], pick[:, 0], pick[:, 1], ALU.add).then_inc(gate_ok, 1)
                dve.wait_ge(gate_ok, c + 1)
                for e in range(E):
                    dve.wait_ge(y_mm, c * E + e + 1)
                    if e:
                        dve.wait_ge(acc_ok, c * E + e)
                    for j in range(4):
                        y = p_y[e % 2][:, j * 128:(j + 1) * 128]
                        if e == 0:
                            ins = dve.tensor_scalar(acc[:, j, :], y, gate[:, j, e:e + 1], None, ALU.mult)
                        else:
                            ins = dve.scalar_tensor_tensor(acc[:, j, :], y, gate[:, j, e:e + 1], acc[:, j, :], ALU.mult, ALU.add)
                    ins.then_inc(acc_ok, 1)
                dve.wait_ge(out_mm, c + 1)
                dve.tensor_tensor(x1c[:], p_t[:], xT[:, bass.ds(c * CH, CH)], ALU.add).then_inc(x1_ok, 1)
                dve.wait_ge(x1_ok, c + 1)
                link_c(dve.tensor_copy(x1[:, bass.ds(c * CH, CH)], x1c[:]))
                dve.wait_ge(xw_mm, c * 4 + 4)


def lstm(nc, io, hs, lstm_xw):
    ctx = ExitStack()
    with ctx:
        def sb(name, shape, dt=F32):
            return ctx.enter_context(nc.sbuf_tensor(name, shape, dt))

        def sem(name):
            return ctx.enter_context(nc.semaphore(name))

        wh = sb("wh", [128, 512])
        whr = sb("whr", [128, 512])
        whp = sb("whp", [128, 3, 512], BF16)
        idn = sb("idn", [128, 128])
        h = sb("h", [128, 2, B])
        hr = sb("hr", [128, B])
        hp = sb("hp", [128, 3, B], BF16)
        sig = sb("sig", [128, 3 * B])
        cand = sb("cand", [128, B])
        ig = sb("ig", [128, B])
        fc = sb("fc", [128, B])
        cell = sb("cell", [128, B])
        tc = sb("tc", [128, B])
        gates = [ctx.enter_context(nc.psum_tensor(f"gates{i}", [128, 512], F32)) for i in range(2)]

        in_h, wprep = sem("in_h"), sem("wprep")
        seed_mm, gates_mm = sem("seed_mm"), sem("gates_mm")
        sig_ok, cand_ok, tc_ok = sem("sig_ok"), sem("cand_ok"), sem("tc_ok")
        cell_ch, cell_ok, h_ch, h1_ok, h2_ok, h3_ok, hs_ok = (
            sem("cell_ch"), sem("cell_ok"), sem("h_ch"), sem("h1_ok"), sem("h2_ok"), sem("h3_ok"), sem("hs_ok"))
        hfull = sem("hfull")

        block = ctx.enter_context(nc.Block())

        @block.sync
        def _(sp):
            sp.dma_start(wh[:], io["wh"]).then_inc(in_h, 16)
            sp.dma_start(h[:, 1, :], io["condT"]).then_inc(in_h, 16)
            sp.dma_start(idn[:], io["ident"]).then_inc(in_h, 16)

        @block.tensor
        def _(pe):
            pe.wait_ge(in_h, 48)

            def step(t, bank, first):
                if not first:
                    pe.wait_ge(cand_ok, t - 1)
                pe.matmul(gates[bank][:, 0:4 * B], idn[:], lstm_xw[:, bass.ds(t * 4 * B, 4 * B)], start=True, stop=False)
                for ready, k, parts in ((h1_ok, 0, (0, 1, 2)), (h2_ok, 1, (0, 1)), (h3_ok, 2, (0,))):
                    pe.wait_ge(ready, t + 1)
                    for w in parts:
                        for g in range(4):
                            last = pe.matmul(gates[bank][:, g * B:(g + 1) * B], whp[:, w, g * 128:(g + 1) * 128], hp[:, k, :],
                                             start=False, stop=(k == 2 and g == 3))
                last.then_inc(gates_mm, 1)

            for t in range(2):
                step(t, t % 2, True)
            for t in range(2, UNR):
                step(t, t % 2, False)
            with pe.Fori(1, T // UNR) as i:
                t0 = i * UNR
                for j in range(UNR):
                    step(t0 + j, j % 2, False)

        @block.scalar
        def _(act):
            def step(t, bank, first):
                act.wait_ge(gates_mm, t + 1)
                act.activation(cand[:], gates[bank][:, 3 * B:4 * B], ACT.Tanh)
                act.activation(sig[:], gates[bank][:, 0:3 * B], ACT.Sigmoid).then_inc(cand_ok, 1)
                act.wait_ge(cell_ok, t + 1)
                act.activation(tc[:], cell[:], ACT.Tanh).then_inc(tc_ok, 1)

            act.preload_act_table_set("sigmoid_and_others")
            with act.Fori(0, T // UNR) as i:
                t0 = i * UNR
                for j in range(UNR):
                    step(t0 + j, j % 2, False)

        @block.vector
        def _(dve):
            done = [0]

            def link(ins):
                done[0] += 1
                ins.then_inc(wprep, 1)
                dve.wait_ge(wprep, done[0])

            dve.wait_ge(in_h, 48)
            link(dve.memset(cell[:], 0.0))
            link(dve.tensor_copy(whp[:, 0, :], wh[:]))
            link(dve.tensor_tensor(whr[:], wh[:], whp[:, 0, :], ALU.subtract))
            link(dve.tensor_copy(whp[:, 1, :], whr[:]))
            link(dve.tensor_tensor(whr[:], whr[:], whp[:, 1, :], ALU.subtract))
            link(dve.tensor_copy(whp[:, 2, :], whr[:]))
            link(dve.tensor_copy(hp[:, 0, :], h[:, 1, :]))
            dve.nop().then_inc(h1_ok, 1)
            link(dve.tensor_tensor(hr[:], h[:, 1, :], hp[:, 0, :], ALU.subtract))
            link(dve.tensor_copy(hp[:, 1, :], hr[:]))
            dve.nop().then_inc(h2_ok, 1)
            link(dve.tensor_tensor(hp[:, 2, :], hr[:], hp[:, 1, :], ALU.subtract))
            dve.nop().then_inc(h3_ok, 1)

            def step(t, buf):
                dve.wait_ge(cand_ok, t + 1)
                dve.tensor_tensor(fc[:], sig[:, B:2 * B], cell[:], ALU.mult)
                dve.tensor_tensor(ig[:], sig[:, 0:B], cand[:], ALU.mult).then_inc(cell_ch, 1)
                dve.wait_ge(cell_ch, t + 1)
                dve.tensor_tensor(cell[:], fc[:], ig[:], ALU.add).then_inc(cell_ok, 1)
                dve.wait_ge(tc_ok, t + 1)
                o = sig[:, 2 * B:3 * B]
                dve.tensor_tensor(hp[:, 0, :], o, tc[:], ALU.mult).then_inc(h1_ok, 1)
                dve.tensor_tensor(h[:, buf, :], o, tc[:], ALU.mult).then_inc(hfull, 1)
                dve.wait_ge(hfull, t + 1)
                dve.tensor_tensor(hp[:, 1, :], h[:, buf, :], hp[:, 0, :], ALU.subtract).then_inc(h2_ok, 1)
                dve.tensor_tensor(hr[:], h[:, buf, :], hp[:, 0, :], ALU.subtract).then_inc(h_ch, 1)
                dve.wait_ge(h_ch, t + 1)
                dve.tensor_tensor(hp[:, 2, :], hr[:], hp[:, 1, :], ALU.subtract).then_inc(h3_ok, 1)

            with dve.Fori(0, T // UNR) as i:
                t0 = i * UNR
                for j in range(UNR):
                    step(t0 + j, j % 2)
                    dve.wait_ge(hs_ok, t0 + j + 1)

        @block.gpsimd
        def _(pool):
            hs_bt = hs[:].rearrange("p (b t) -> p b t", t=T)
            with pool.Fori(0, T // UNR) as i:
                t0 = i * UNR
                for j in range(UNR):
                    pool.wait_ge(hfull, t0 + j + 1)
                    pool.tensor_copy(hs_bt[:, :, bass.ds(t0 + j, 1)], h[:, j % 2, :].unsqueeze(2)).then_inc(hs_ok, 1)


def transformer(nc, io, x, x1):
    ctx = ExitStack()
    with ctx:
        def sb(name, shape, dt=F32):
            return ctx.enter_context(nc.sbuf_tensor(name, shape, dt))

        def sem(name):
            return ctx.enter_context(nc.semaphore(name))

        NS = LAYERS * B

        ident = sb("t_ident", [128, 128])
        identb = sb("t_identb", [128, 128], BF16)
        maskf = sb("t_maskf", [128, TILES * 2 * 2 * WIN])
        ones = sb("t_ones", [128, 128])
        mask = sb("t_mask", [128, TILES * 2 * 2 * WIN], BF16)
        rot = sb("t_rot", [128, TILES, 2, 2, HD])
        scl = sb("t_scl", [128, LAYERS, 2, 2, HD])
        tab = sb("t_tab", [128, LAYERS * TILES * 2 * 2 * HD])
        wqkv = sb("t_wqkv", [128, 2 * GROUPS * GC])
        wo = sb("t_wo", [128, 8, 128])
        w1 = sb("t_w1", [128, 2 * FCH, FW])
        b1 = sb("t_b1", [128, 2 * FCH])
        w2 = sb("t_w2", [FW, FCH, 128])
        b2 = sb("t_b2", [128, 1])
        lnp = sb("t_lnp", [128, 2])
        ln_bias = sb("t_eps", [128, 1])

        xs = sb("t_xs", [128, T])
        sq = sb("t_sq", [128, TILES, QK])
        ss = sb("t_ss", [128, TILES, 2 * GH])
        lns = sb("t_lns", [128, TILES, 2 * GH])
        ers = sb("t_ers", [128, TILES, 2 * GH])
        nt = sb("t_nt", [128, TILES, 2 * GH])
        rn = sb("t_rn", [128, TILES, 2 * GH])
        cosp = sb("t_cosp", [128, TILES, QK])
        sinp = sb("t_sinp", [128, TILES, QK])
        qkn = sb("t_qkn", [128, TILES, QK])
        vn = sb("t_vn", [128, GROUPS, TILES, VC])
        vp = sb("t_vp", [128, GROUPS, TILES, VC])
        qT = sb("t_qT", [128, 2, T])
        kT = sb("t_kT", [128, 2, WIN + T])
        smax = sb("t_smax", [128, 2, TILES, 2])
        ssub = sb("t_ssub", [128, 2, TILES, 2, 2 * WIN])
        prob = sb("t_prob", [128, 2, TILES, 2, 2 * WIN])
        psm = sb("t_psm", [128, 2, TILES, 2])
        pinv = sb("t_pinv", [128, 2, TILES, 2])
        cT = sb("t_cT", [128, 16, WIN])
        pT = sb("t_pT", [128, 2, 16, 128])
        oT = sb("t_oT", [128, 2, T])

        xf = sb("t_xf", [128, T])
        xc = sb("t_xc", [128, T])
        xq = sb("t_xq", [128, T])
        var = sb("t_var", [128, T])
        lnv = sb("t_lnv", [128, T])
        erv = sb("t_erv", [128, T])
        nv = sb("t_nv", [128, T])
        xh = sb("t_xh", [128, T])
        xn = sb("t_xn", [128, T])
        fa = sb("t_fa", [FW, FCH, T])
        fg = sb("t_fg", [FW, FCH, T])
        fh = sb("t_fh", [FW, FCH, T])

        def bank(name):
            return ctx.enter_context(nc.psum_tensor(name, [128, 512], F32))

        p_qk = [bank("p_qk0"), bank("p_qk1")]
        p_v, p_a, p_b, p_o = bank("p_v"), bank("p_a"), bank("p_b"), bank("p_o")
        p_s = [bank("p_s0"), bank("p_s1")]

        in_c, in_w = sem("in_c"), sem("in_w")
        in_wo, in_ln, in_w1, in_w2 = sem("in_wo"), sem("in_ln"), sem("in_w1"), sem("in_w2")
        tab_ch, tab_ok, zero_ok = sem("tab_ch"), sem("tab_ok"), sem("zero_ok")
        xs_ok, qk_mm, v_mm, sq_ok, v_ok = sem("xs_ok"), sem("qk_mm"), sem("v_mm"), sem("sq_ok"), sem("v_ok")
        vp_ok = [sem(f"vp_ok{g}") for g in range(GROUPS)]
        rot_ok, ss_ok, ln_ok, er_ok, n_ch, rn_ok = (
            sem("rot_ok"), sem("ss_ok"), sem("ln_ok"), sem("er_ok"), sem("n_ch"), sem("rn_ok"))
        add_ok, qkn_ok = sem("add_ok"), sem("qkn_ok")
        qT_mm, kT_mm, qT_ok, kT_ok = sem("qT_mm"), sem("kT_mm"), sem("qT_ok"), sem("kT_ok")
        s_mm, mx_ch, sub_ok, exp_ok, inv_ch, cT_ok, pT_ok = (
            sem("s_mm"), sem("mx_ch"), sem("sub_ok"), sem("exp_ok"), sem("inv_ch"), sem("cT_ok"), sem("pT_ok"))
        pv_mm, oT_ok, wo_mm, x_ok = sem("pv_mm"), sem("oT_ok"), sem("wo_mm"), sem("x_ok")
        xf_ok, mu_mm, xc_ok, xq_ok, var_mm = sem("xf_ok"), sem("mu_mm"), sem("xc_ok"), sem("xq_ok"), sem("var_mm")
        var_ok, lnv_ok, erv_ok, nv_ch, xh_ok, xn_ok = (
            sem("var_ok"), sem("lnv_ok"), sem("erv_ok"), sem("nv_ch"), sem("xh_ok"), sem("xn_ok"))
        up_mm, up_ok, gelu_ok, fh_ok, down_mm, ffn_ok = (
            sem("up_mm"), sem("up_ok"), sem("gelu_ok"), sem("fh_ok"), sem("down_mm"), sem("ffn_ok"))
        out_ok, stored = sem("out_ok"), sem("stored")

        block = ctx.enter_context(nc.Block())

        def whole(n):
            return isinstance(n, int)

        def live(n):
            return not whole(n) or 0 <= n < NS

        def has(n, g, back):
            return not whole(n) or 0 <= 4 * n + g - back < 4 * NS

        def loads(n, back):
            return (n - back) // B + 1 if whole(n) else (n + (B - back)) >> 3

        def layer(n):
            if whole(n):
                return n // B
            return nc.s_assert_within(n >> 3, 0, LAYERS - 1, skip_runtime_bounds_check_because="n is below LAYERS * B")

        def schedule(eng, unit):
            for n in range(3):
                for g in range(GROUPS):
                    unit(n, g)
            with eng.Fori(3, NS) as n:
                for g in range(GROUPS):
                    unit(n, g)
            for n in range(NS, NS + 2):
                for g in range(GROUPS):
                    unit(n, g)

        def seq(n, p0, p1, t0, t1):
            off = (n % B if whole(n) else n & (B - 1)) * T + t0
            return x[p0:p1, bass.ds(off, t1 - t0)]


        @block.sync
        def _(sp):
            for dst, name in ((ident, "ident"), (ones, "ones"), (maskf, "mask"), (rot, "rot")):
                sp.dma_start(dst[:], io[name]).then_inc(in_c, 16)
            for k, name in ((0, "q_scale"), (1, "k_scale")):
                s = io[name]
                sp.dma_start(scl[:, :, 0, k, :], s.partition_broadcast(128)).then_inc(in_c, 16)
                sp.dma_start(scl[:, :, 1, k, 0:32], s[:, 32:64].partition_broadcast(128)).then_inc(in_c, 16)
                sp.dma_start(scl[:, :, 1, k, 32:64], s[:, 0:32].partition_broadcast(128)).then_inc(in_c, 16)
            W = GROUPS * GC
            sp.dma_start(wqkv[:, 0:W], io["wqkv"][:, 0:W]).then_inc(in_w, 16)
            small = [(in_wo, wo, "wo"), (in_ln, lnp, "lnp"), (in_w1, w1, "w1"),
                     (in_w1, b1, "b1"), (in_w2, w2, "w2"), (in_w2, b2, "b2")]

            def width(name):
                return io[name].shape[1] // LAYERS

            def load(at, which):
                for s, dst, name in small:
                    if s is which:
                        flat = dst[:] if len(dst.shape) == 2 else dst[:].rearrange("p a b -> p (a b)")
                        sp.dma_start(flat, io[name][:, bass.ds(at[name], width(name))],
                                     allow_slow_non_contiguous=width(name) == 1).then_inc(s, 16)

            for s in (in_wo, in_ln, in_w1, in_w2):
                load({name: 0 for _, _, name in small}, s)
            sp.wait_ge(in_w, 16)
            sp.dma_start(wqkv[:, W:2 * W], io["wqkv"][:, W:2 * W]).then_inc(in_w, 16)

            def shift_v(n, g):
                sp.wait_ge(v_ok, 4 * n + g + 1)
                sp.dma_start(vp[WIN:128, g, :, :], vn[0:128 - WIN, g, :, :]).then_inc(vp_ok[g], 16)
                sp.dma_start(vp[0:WIN, g, 1:TILES, :], vn[128 - WIN:128, g, 0:TILES - 1, :]).then_inc(vp_ok[g], 16)

            with sp.Fori(0, B) as b:
                for g in range(GROUPS):
                    shift_v(b, g)
            for l in range(1, LAYERS):
                first = l * B
                at = {name: l * width(name) for _, _, name in small}
                for g in range(GROUPS):
                    shift_v(first, g)
                    if g == 2:
                        sp.wait_ge(wo_mm, 4 * first)
                        load(at, in_wo)
                        if l + 1 < LAYERS:
                            sp.wait_ge(v_mm, 4 * first)
                            slot = (l + 1) % 2 * W
                            sp.dma_start(wqkv[:, slot:slot + W], io["wqkv"][:, (l + 1) * W:(l + 2) * W]).then_inc(in_w, 16)
                for g in range(GROUPS):
                    shift_v(first + 1, g)
                    if g == 2:
                        sp.wait_ge(xn_ok, first)
                        load(at, in_ln)
                    if g == 3:
                        sp.wait_ge(up_ok, first * FCH)
                        load(at, in_w1)
                for g in range(GROUPS):
                    shift_v(first + 2, g)
                    if g == 0:
                        sp.wait_ge(ffn_ok, first)
                        load(at, in_w2)
                with sp.Fori(first + 3, first + B) as n:
                    for g in range(GROUPS):
                        shift_v(n, g)
            sp.wait_ge(out_ok, 1)
            sp.dma_start(io["out"], x[:]).then_inc(stored, 16)
            sp.wait_ge(stored, 16)

        @block.tensor
        def _(pe):
            pe.wait_ge(in_c, 16 * 10)
            pe.wait_ge(zero_ok, 1)

            def project(n, g):
                if g == 0:
                    pe.wait_ge(xs_ok, n + 1)
                    pe.wait_ge(in_w, 16 * loads(n, 0))
                base = g * GC if whole(n) else ((n >> 3) & 1) * (GROUPS * GC) + g * GC
                before = has(n, g, 1)
                for j in range(TILES):
                    if before:
                        pe.wait_ge(rot_ok, (4 * n + g) * TILES + j - TILES + 1)
                    pe.matmul(p_qk[j][:], xs[:, j * 128:(j + 1) * 128], wqkv[:, bass.ds(base, QK)],
                              start=True, stop=True).then_inc(qk_mm, 1)
                    if j == 0 and before:
                        pe.wait_ge(v_ok, 4 * n + g)
                        if g == 2 and live(n - 2):
                            pe.wait_ge(up_ok, FCH * (n - 2) + 1)
                        if g == 0 and live(n - 3):
                            pe.wait_ge(ffn_ok, n - 2)
                    last = pe.matmul(p_v[:, j * VC:(j + 1) * VC], xs[:, j * 128:(j + 1) * 128],
                                     wqkv[:, bass.ds(base + QK, VC)], start=True, stop=True)
                last.then_inc(v_mm, 1)

            def turn(n, g):
                u = 4 * n + g - 1
                if has(n, g, 2):
                    pe.wait_ge(qT_ok, u)
                if has(n, g, 4):
                    pe.wait_ge(x_ok, u - 2)
                if g == 0 and live(n - 2):
                    pe.wait_ge(xc_ok, n - 1)
                if g == 1 and live(n - 2):
                    pe.wait_ge(var_ok, n - 1)
                if g == 2 and live(n - 2):
                    pe.wait_ge(up_ok, FCH * (n - 2) + 2)
                if g == 3 and live(n - 2):
                    pe.wait_ge(up_ok, FCH * (n - 2) + 3)
                pe.wait_ge(qkn_ok, (u + 1) * TILES)
                for c, bank_, s in ((0, p_a, qT_mm), (1, p_b, kT_mm)):
                    for hp in range(2):
                        for j in range(TILES):
                            at = c * VC + hp * 128
                            last = pe.transpose(bank_[:, hp * T + j * 128:hp * T + (j + 1) * 128],
                                                qkn[:, j, at:at + 128], ident[:])
                    last.then_inc(s, 1)

            def values(n, g):
                u = 4 * n + g - 3
                s = (g + 1) % GROUPS
                pe.wait_ge(pT_ok, u + 1)
                pe.wait_ge(vp_ok[s], 32 * n + 32 if g == 3 else 32 * n)
                if has(n, g, 4):
                    pe.wait_ge(oT_ok, u)
                for j in range(TILES):
                    for hp in range(2):
                        for half, v in ((0, vp), (1, vn)):
                            for par in range(2):
                                h = 2 * hp + par
                                i = 2 * ((par * TILES + j) * 2 + hp) + half
                                o = p_o[64 * par:64 * par + 64, hp * T + j * 128:hp * T + (j + 1) * 128]
                                last = pe.matmul(o, v[:, s, j, h * HD:(h + 1) * HD], pT[:, (g + 1) % 2, i, :],
                                                 start=(half == 0), stop=(half == 1), skip_group_check=True)
                last.then_inc(pv_mm, 1)

            def scores(n, g):
                u = 4 * n + g - 1
                pe.wait_ge(qT_ok, u + 1)
                pe.wait_ge(kT_ok, u + 1)
                if has(n, g, 2):
                    pe.wait_ge(sub_ok, u)
                for par in range(2):
                    rows = slice(64 * par, 64 * par + 64)
                    pe.matmul(p_s[par][:, 0:256], identb[:], mask[:], start=True, stop=False, skip_group_check=True)
                    for j in range(TILES):
                        for hp in range(2):
                            for w in range(4):
                                col = (j * 2 + hp) * 2 * WIN
                                t = j * 128 + w * WIN
                                last = pe.matmul(p_s[par][w * WIN:(w + 1) * WIN, col:col + 2 * WIN],
                                                 qT[rows, hp, t:t + WIN], kT[rows, hp, t:t + 2 * WIN],
                                                 start=False, stop=True, skip_group_check=True)
                last.then_inc(s_mm, 1)

            def out_proj(n, g):
                u = 4 * n + g - 3
                pe.wait_ge(in_wo, 16 * loads(n, 1 if g < 3 else 0))
                pe.wait_ge(oT_ok, u + 1)
                if has(n, g, 1):
                    pe.wait_ge(kT_ok, u + 3)
                else:
                    pe.wait_ge(x_ok, u)
                for hp in range(2):
                    last = pe.matmul(p_b[:, 0:T], wo[:, (2 * (g - 3) + hp) % 8, :], oT[:, hp, :],
                                     start=(hp == 0), stop=(hp == 1))
                last.then_inc(wo_mm, 1)

            def q_out(n, g):
                u = 4 * n + g
                pe.wait_ge(qT_ok, min(u, 4 * NS) if whole(n) else u)

            def v_out(n, g):
                u = 4 * n + g + 1
                pe.wait_ge(v_ok, min(u, 4 * NS) if whole(n) else u)

            def up(m, c, bank_):
                for k in range(2):
                    last = pe.matmul(bank_[0:FW, k * T:(k + 1) * T], w1[:, k * FCH + c, :], xn[:], start=True, stop=True)
                last.then_inc(up_mm, 1)

            def feed_forward(n, g):
                if g == 0 and live(n - 2):
                    pe.wait_ge(xq_ok, n - 1)
                    q_out(n, g)
                    pe.wait_ge(xc_ok, n - 1)
                    pe.matmul(p_a[:, 0:T], ones[:], xq[:], start=True, stop=True).then_inc(var_mm, 1)
                if g == 1 and live(n - 2):
                    pe.wait_ge(xn_ok, n - 1)
                    pe.wait_ge(in_w1, 32 * loads(n, 2))
                    v_out(n, g)
                    up(n - 2, 0, p_v)
                    q_out(n, g)
                    pe.wait_ge(var_ok, n - 1)
                    up(n - 2, 1, p_a)
                if g == 2 and live(n - 2):
                    q_out(n, g)
                    pe.wait_ge(up_ok, FCH * (n - 2) + 2)
                    up(n - 2, 2, p_a)
                if g == 3 and live(n - 1):
                    pe.wait_ge(xf_ok, n)
                    q_out(n, g)
                    if live(n - 2):
                        pe.wait_ge(up_ok, FCH * (n - 1))
                    pe.matmul(p_a[:, 0:T], ones[:], xf[:], start=True, stop=True).then_inc(mu_mm, 1)
                if g == 3 and live(n - 2):
                    pe.wait_ge(fh_ok, n - 1)
                    pe.wait_ge(in_w2, 32 * loads(n, 2))
                    v_out(n, g)
                    for c in range(FCH):
                        last = pe.matmul(p_v[:, 0:T], w2[:, c, :], fh[:, c, :], start=(c == 0), stop=(c == FCH - 1))
                    last.then_inc(down_mm, 1)

            def unit(n, g):
                if has(n, g, 0):
                    project(n, g)
                if has(n, g, 1):
                    turn(n, g)
                if has(n, g, 3):
                    values(n, g)
                if has(n, g, 1):
                    scores(n, g)
                if has(n, g, 3):
                    out_proj(n, g)
                feed_forward(n, g)

            schedule(pe, unit)

        @block.scalar
        def _(act):
            act.preload_act_table_set("natural_log_exp_and_others")
            act.wait_ge(zero_ok, 1)

            def copies_in(n, g):
                u = 4 * n + g
                for j in range(TILES):
                    act.wait_ge(qk_mm, u * TILES + j + 1)
                    if has(n, g, 1):
                        act.wait_ge(ss_ok, u)
                    act.activation(sq[:, j, :], p_qk[j][:], ACT.Square).then_inc(sq_ok, 1)
                act.wait_ge(v_mm, u + 1)
                if live(n - 1):
                    act.wait_ge(pv_mm, u - 3)
                act.activation(vn[:, g, :, :].rearrange("p j c -> p (j c)"), p_v[:], ACT.Copy).then_inc(v_ok, 1)

            def inverse_norms(n, g):
                u = 4 * n + g
                act.wait_ge(ss_ok, u + 1)
                act.activation(lns[:], ss[:], ACT.Ln, scale=RS * RS).then_inc(ln_ok, 1)
                act.wait_ge(ln_ok, u + 1)
                if has(n, g, 1):
                    act.wait_ge(rn_ok, u)
                act.activation(ers[:], lns[:], ACT.Exp, scale=-0.5).then_inc(er_ok, 1)

            def turned(n, g):
                u = 4 * n + g - 1
                act.wait_ge(qT_mm, u + 1)
                if has(n, g, 2):
                    act.wait_ge(s_mm, u)
                act.activation(qT[:].rearrange("p a t -> p (a t)"), p_a[:], ACT.Copy).then_inc(qT_ok, 1)
                act.wait_ge(kT_mm, u + 1)
                act.activation(kT[:, :, WIN:WIN + T], p_b[:].rearrange("p (a t) -> p a t", a=2), ACT.Copy).then_inc(kT_ok, 1)

            def exps(n, g):
                u = 4 * n + g - 1
                act.wait_ge(sub_ok, u + 1)
                if has(n, g, 2):
                    act.wait_ge(cT_ok, u)
                act.activation(prob[:], ssub[:], ACT.Exp).then_inc(exp_ok, 1)

            def spread(n, g):
                u = 4 * n + g - 2
                act.wait_ge(cT_ok, u + 1)
                if has(n, g, 4):
                    act.wait_ge(pv_mm, u - 1)
                for w in range(4):
                    rows = slice(w * WIN, (w + 1) * WIN)
                    ins = act.activation(pT[rows, g % 2, :, w * WIN:(w + 1) * WIN], cT[rows, :, :], ACT.Copy)
                ins.then_inc(pT_ok, 1)

            def turned_out(n, g):
                u = 4 * n + g - 3
                act.wait_ge(pv_mm, u + 1)
                if has(n, g, 4):
                    act.wait_ge(wo_mm, u)
                act.activation(oT[:].rearrange("p a t -> p (a t)"), p_o[:], ACT.Copy).then_inc(oT_ok, 1)

            def up_out(m, c, bank_):
                act.wait_ge(up_mm, FCH * m + c + 1)
                act.wait_ge(in_w1, 32 * m_loads[0])
                for k, dst in ((0, fa), (1, fg)):
                    ins = act.activation(dst[:, c, :], bank_[0:FW, k * T:(k + 1) * T], ACT.Identity,
                                         bias=b1[0:FW, k * FCH + c:k * FCH + c + 1])
                ins.then_inc(up_ok, 1)

            m_loads = [0]

            def feed_forward(n, g):
                if g == 3 and live(n - 1):
                    m = n - 1
                    act.wait_ge(x_ok, 4 * n)
                    if live(n - 2):
                        act.wait_ge(xc_ok, m)
                    act.activation(xf[0:64, :], seq(m, 0, 64, 0, T), ACT.Copy)
                    act.activation(xf[64:128, 1:T], seq(m, 64, 128, 0, T - 1), ACT.Copy).then_inc(xf_ok, 1)
                if g == 1 and live(n - 2):
                    m = n - 2
                    act.wait_ge(xh_ok, m + 1)
                    act.wait_ge(in_ln, 16 * loads(n, 2))
                    act.activation(xn[:], xh[:], ACT.Identity, bias=lnp[:, 1:2], scale=lnp[:, 0:1]).then_inc(xn_ok, 1)

            def feed_forward_late(n, g):
                m_loads[0] = loads(n, 2)
                if g == 0 and live(n - 2):
                    m = n - 2
                    act.wait_ge(var_mm, m + 1)
                    act.activation(var[:], p_a[:, 0:T], ACT.Identity, bias=ln_bias[:]).then_inc(var_ok, 1)
                    act.wait_ge(var_ok, m + 1)
                    act.activation(lnv[:], var[:], ACT.Ln).then_inc(lnv_ok, 1)
                    act.wait_ge(lnv_ok, m + 1)
                    act.activation(erv[:], lnv[:], ACT.Exp, scale=-0.5).then_inc(erv_ok, 1)
                if g == 1 and live(n - 2):
                    if live(n - 3):
                        act.wait_ge(fh_ok, n - 2)
                    up_out(n - 2, 0, p_v)
                    up_out(n - 2, 1, p_a)
                if g == 2 and live(n - 2):
                    up_out(n - 2, 2, p_a)
                    act.wait_ge(up_ok, FCH * (n - 1))
                    flat = fg[:].rearrange("p c t -> p (c t)")
                    act.activation(flat, flat, ACT.Gelu).then_inc(gelu_ok, 1)
                    act.preload_act_table_set("natural_log_exp_and_others")

            def unit(n, g):
                if has(n, g, 0):
                    copies_in(n, g)
                if has(n, g, 1):
                    turned(n, g)
                if has(n, g, 2):
                    spread(n, g)
                if has(n, g, 3):
                    turned_out(n, g)
                if has(n, g, 0):
                    inverse_norms(n, g)
                feed_forward(n, g)
                if has(n, g, 1):
                    exps(n, g)
                feed_forward_late(n, g)

            schedule(act, unit)

        @block.vector
        def _(dve):
            dve.memset(vp[0:WIN, :, 0:1, :], 0.0)
            dve.memset(kT[:, :, 0:WIN], 0.0)
            dve.memset(pT[:], 0.0)
            dve.memset(xs[64:128, 0:1], 0.0)
            dve.memset(xf[64:128, 0:1], 0.0)
            dve.memset(ln_bias[:], 1e-5)
            dve.wait_ge(in_c, 16 * 10)
            dve.tensor_copy(identb[:], ident[:])
            dve.tensor_copy(mask[:], maskf[:]).then_inc(zero_ok, 1)
            dve.wait_ge(zero_ok, 1)

            def shift_in(n):
                dve.tensor_copy(xs[0:64, :], seq(n, 0, 64, 0, T))
                dve.tensor_copy(xs[64:128, 1:T], seq(n, 64, 128, 0, T - 1)).then_inc(xs_ok, 1)

            shift_in(0)
            dve.wait_ge(tab_ok, 1)

            def rotate(n, g):
                u = 4 * n + g
                lay = layer(n) * (TILES * 256)
                if has(n, g, 1):
                    dve.wait_ge(qkn_ok, u * TILES)
                for j in range(TILES):
                    dve.wait_ge(sq_ok, u * TILES + j + 1)
                    if j == 0 and has(n, g, 1):
                        dve.wait_ge(er_ok, u)
                    q = p_qk[j][:].rearrange("p (k h d) -> p k h d", k=2, h=GH)
                    c = cosp[:, j, :].rearrange("p (k h d) -> p k h d", k=2, h=GH)
                    s = sinp[:, j, :].rearrange("p (k h d) -> p k h d", k=2, h=GH)

                    def table(which, d0, d1):
                        t = tab[:, bass.ds(lay + j * 256 + which * 128, 128)].rearrange("p (k d) -> p k d", k=2)
                        return t[:, :, d0:d1].unsqueeze(2).broadcast_to([128, 2, GH, d1 - d0])

                    dve.tensor_tensor(c, q, table(0, 0, HD), ALU.mult)
                    dve.tensor_tensor(s[:, :, :, 0:32], q[:, :, :, 32:64], table(1, 0, 32), ALU.mult)
                    dve.tensor_tensor(s[:, :, :, 32:64], q[:, :, :, 0:32], table(1, 32, 64), ALU.mult).then_inc(rot_ok, 1)
                    ins = dve.tensor_reduce(ss[:, j, :], sq[:, j, :].rearrange("p (h d) -> p h d", d=HD), AX.X, ALU.add)
                ins.then_inc(n_ch, 1)
                dve.wait_ge(n_ch, 3 * u + 1)
                dve.tensor_scalar(ss[:], ss[:], 1e-24, None, ALU.max).then_inc(ss_ok, 1)

            def norms(n, g):
                u = 4 * n + g
                dve.wait_ge(er_ok, u + 1)
                dve.scalar_tensor_tensor(nt[:], ers[:], RS * RS, ers[:], ALU.mult, ALU.mult).then_inc(n_ch, 1)
                dve.wait_ge(n_ch, 3 * u + 2)
                dve.scalar_tensor_tensor(nt[:], nt[:], -0.5, ss[:], ALU.mult, ALU.mult).then_inc(n_ch, 1)
                dve.wait_ge(n_ch, 3 * u + 3)
                dve.scalar_tensor_tensor(rn[:], nt[:], 1.5, ers[:], ALU.add, ALU.mult).then_inc(rn_ok, 1)

            def softmax(n, g):
                u = 4 * n + g - 1
                dve.wait_ge(s_mm, u + 1)
                s = [p_s[par][:, 0:256].rearrange("p (q c) -> p q c", c=2 * WIN) for par in range(2)]
                m = smax[:].rearrange("p a j b -> p a (j b)")
                for par in range(2):
                    ins = dve.tensor_reduce(m[:, par, :], s[par], AX.X, ALU.max)
                ins.then_inc(mx_ch, 1)
                dve.wait_ge(mx_ch, u + 1)
                if has(n, g, 2):
                    dve.wait_ge(exp_ok, u)
                z = ssub[:].rearrange("p a j b c -> p a (j b) c")
                for par in range(2):
                    ins = dve.tensor_tensor(z[:, par], s[par], m[:, par, :].unsqueeze(2).broadcast_to([128, 4, 2 * WIN]),
                                            ALU.subtract)
                ins.then_inc(sub_ok, 1)

            def divide(n, g):
                u = 4 * n + g - 1
                dve.wait_ge(exp_ok, u + 1)
                p = prob[:].rearrange("p a j b c -> p (a j b) c")
                dve.tensor_reduce(psm[:].rearrange("p a j b -> p (a j b)"), p, AX.X, ALU.add).then_inc(inv_ch, 1)
                dve.wait_ge(inv_ch, 3 * u + 1)
                dve.reciprocal(pinv[:], psm[:]).then_inc(inv_ch, 1)
                dve.wait_ge(inv_ch, 3 * u + 2)
                inv = pinv[:].rearrange("p a j b -> p (a j b)").unsqueeze(2).broadcast_to([128, 8, 2 * WIN])
                dve.tensor_tensor(p, p, inv, ALU.mult).then_inc(inv_ch, 1)
                dve.wait_ge(inv_ch, 3 * u + 3)
                if has(n, g, 2):
                    dve.wait_ge(pT_ok, u)
                dve.transpose(cT[:].rearrange("p i c -> p (i c)"), prob[:].rearrange("p a j b c -> p (a j b c)")).then_inc(cT_ok, 1)

            def residual(n, g):
                u = 4 * n + g - 3
                m = n - 1 if g < 3 else n
                dve.wait_ge(wo_mm, u + 1)
                dst = seq(m, 0, 128, 0, T)
                dve.tensor_tensor(dst, dst, p_b[:, 0:T], ALU.add).then_inc(x_ok, 1)

            def feed_forward_early(n, g):
                if g == 1 and live(n - 2):
                    m = n - 2
                    dve.wait_ge(erv_ok, m + 1)
                    dve.tensor_tensor(nv[:], erv[:], erv[:], ALU.mult).then_inc(nv_ch, 1)
                    dve.wait_ge(nv_ch, 3 * m + 1)
                    dve.scalar_tensor_tensor(nv[:], nv[:], -0.5, var[:], ALU.mult, ALU.mult).then_inc(nv_ch, 1)
                    dve.wait_ge(nv_ch, 3 * m + 2)
                    dve.scalar_tensor_tensor(nv[:], nv[:], 1.5, erv[:], ALU.add, ALU.mult).then_inc(nv_ch, 1)
                    dve.wait_ge(nv_ch, 3 * m + 3)
                    if live(n - 3):
                        dve.wait_ge(xn_ok, m)
                    dve.tensor_tensor(xh[:], xc[:], nv[:], ALU.mult).then_inc(xh_ok, 1)

            def feed_forward_late(n, g):
                if g == 3 and live(n - 1):
                    m = n - 1
                    dve.wait_ge(mu_mm, m + 1)
                    dve.tensor_tensor(xc[:], xf[:], p_a[:, 0:T], ALU.subtract).then_inc(xc_ok, 1)
                if g == 3 and live(n - 2):
                    m = n - 2
                    dve.wait_ge(down_mm, m + 1)
                    dve.wait_ge(in_w2, 32 * loads(n, 2))
                    dst = seq(m, 0, 128, 0, T)
                    dve.scalar_tensor_tensor(dst, p_v[:, 0:T], b2[:], dst, ALU.add, ALU.add).then_inc(ffn_ok, 1)

            def unit(n, g):
                if has(n, g, 0):
                    rotate(n, g)
                    norms(n, g)
                feed_forward_early(n, g)
                if g == 3 and live(n + 1):
                    dve.wait_ge(v_mm, 4 * n + 4)
                    shift_in(n + 1)
                if has(n, g, 1):
                    softmax(n, g)
                if has(n, g, 3):
                    residual(n, g)
                if has(n, g, 1):
                    divide(n, g)
                feed_forward_late(n, g)

            schedule(dve, unit)
            dve.wait_ge(ffn_ok, NS)
            dve.tensor_tensor(x[:].rearrange("p (b t) -> p b t", b=B), x[:].rearrange("p (b t) -> p b t", b=B),
                              x1[:].rearrange("p (t b) -> p b t", b=B), ALU.add).then_inc(out_ok, 1)

        @block.gpsimd
        def _(pool):
            pool.wait_ge(in_c, 16 * 10)
            for l in range(LAYERS):
                for j in range(TILES):
                    ins = pool.tensor_tensor(tab[:, (l * TILES + j) * 256:(l * TILES + j + 1) * 256], rot[:, j].rearrange("p a b d -> p (a b d)"),
                                             scl[:, l].rearrange("p a b d -> p (a b d)"), ALU.mult)
            ins.then_inc(tab_ok, 1)

            def normalised(n, g):
                u = 4 * n + g
                for j in range(TILES):
                    pool.wait_ge(rot_ok, u * TILES + j + 1)
                    pool.tensor_tensor(cosp[:, j, :], cosp[:, j, :], sinp[:, j, :], ALU.add).then_inc(add_ok, 1)
                pool.wait_ge(rn_ok, u + 1)
                if has(n, g, 1):
                    pool.wait_ge(kT_mm, u)
                for j in range(TILES):
                    pool.wait_ge(add_ok, u * TILES + j + 1)
                    pool.tensor_tensor(qkn[:, j, :].rearrange("p (h d) -> p h d", d=HD),
                                       cosp[:, j, :].rearrange("p (h d) -> p h d", d=HD),
                                       rn[:, j, :].unsqueeze(2).broadcast_to([128, 2 * GH, HD]), ALU.mult).then_inc(qkn_ok, 1)

            def feed_forward(n, g):
                if g == 0 and live(n - 2):
                    m = n - 2
                    pool.wait_ge(xc_ok, m + 1)
                    if live(n - 3):
                        pool.wait_ge(var_mm, m)
                    pool.tensor_tensor(xq[:], xc[:], xc[:], ALU.mult).then_inc(xq_ok, 1)
                if g == 3 and live(n - 2):
                    m = n - 2
                    pool.wait_ge(gelu_ok, m + 1)
                    if live(n - 3):
                        pool.wait_ge(down_mm, m)
                    pool.tensor_tensor(fh[:], fa[:], fg[:], ALU.mult).then_inc(fh_ok, 1)

            def unit(n, g):
                feed_forward(n, g)
                if has(n, g, 0):
                    normalised(n, g)

            schedule(pool, unit)


def program(nc, io):
    with (nc.sbuf_tensor("hs", [128, TOK], F32) as hs, nc.sbuf_tensor("x1", [128, TOK], F32) as x1):
        with nc.sbuf_tensor("lstm_xw", [128, TOK * 4], F32) as lstm_xw:
            spiking_and_experts(nc, io, x1, lstm_xw)
            lstm(nc, io, hs, lstm_xw)
        transformer(nc, io, hs, x1)


def shape_constants():
    f = np.float32
    half = np.arange(0, HD, 2, dtype=f)
    inv_freq = f(1.0) / f(10000.0) ** (half / f(HD))
    t = np.arange(T, dtype=f)
    freqs = np.concatenate([t[:, None] * inv_freq[None, :]] * 2, -1)
    base = (half + f(0.4 * HD)) / f(1.4 * HD)
    power = (t - f(T // 2)) / f(WIN // 2)
    scale = np.concatenate([(base[None, :] ** power[:, None]).astype(f)] * 2, -1)
    cos, sin = np.cos(freqs).astype(f), np.sin(freqs).astype(f)
    sign = np.concatenate([-np.ones(32, f), np.ones(32, f)])
    inv = (f(1.0) / scale).astype(f)
    rot = np.zeros((T, 2, 2, HD), f)
    rot[:, 0, 0] = cos * scale * f(8.0 * RS)
    rot[:, 1, 0] = sign * sin * scale * f(8.0 * RS)
    rot[:, 0, 1] = cos * inv * f(RS)
    rot[:, 1, 1] = sign * sin * inv * f(RS)
    rot = rot.reshape(TILES, 128, 2, 2, HD).transpose(1, 0, 2, 3, 4)
    i = np.arange(128)[:, None]
    c = np.arange(2 * WIN)[None, :]
    ok = np.where(c < WIN, c >= i % WIN, c - WIN <= i % WIN)
    mask = np.zeros((128, TILES, 2, 2 * WIN), f)
    for j in range(TILES):
        first = (i < WIN) & (c < WIN) & (j == 0)
        mask[:, j] = np.where(ok & ~first, 0.0, -1e38)[:, None, :]
    return {
        "ident": np.eye(128, dtype=f), "off_diag": 1 - np.eye(128, dtype=f),
        "ones": np.full((128, 128), 1.0 / D, f),
        "mask": mask.reshape(128, -1), "rot": np.ascontiguousarray(rot),
        "iota": np.tile(np.arange(E, dtype=f), (128, 1)),
    }


def layouts(a):
    out = {}
    out["xT"] = a["x"].transpose(2, 1, 0).reshape(128, TOK)
    out["condT"] = a["cond_1024"].T
    out["wlif"] = a["L0_cond_W"].T
    out["vlif"] = a["L0_cond_V"]
    out["alpha_col"] = a["L0_cond_alpha"].reshape(128, 1)
    out["alpha_row"] = a["L0_cond_alpha"]
    out["wg"] = a["L0_ffn_Wg"]
    out["e_w1"] = a["L0_ffn_W1"].transpose(1, 0, 2).reshape(128, E * EH)
    out["e_b1"] = a["L0_ffn_b1"].reshape(E * HALVES, 128).T
    out["e_w2"] = a["L0_ffn_W2"].reshape(E * HALVES, 128, 128).transpose(1, 0, 2).reshape(128, -1)
    out["e_b2"] = a["L0_ffn_b2"]
    out["wx"] = a["L1_cond_Wx"]
    out["wh"] = a["L1_cond_Wh"]
    out["bx"] = a["L1_cond_b"].reshape(4, 128).T
    w = a["L1_ffn_Wqkv"].reshape(LAYERS, 128, 3, GROUPS, VC)
    out["wqkv"] = w.transpose(1, 0, 3, 2, 4).reshape(128, -1)
    out["q_scale"], out["k_scale"] = a["L1_ffn_q_scale"], a["L1_ffn_k_scale"]
    out["wo"] = a["L1_ffn_Wo"].reshape(LAYERS, 8, 128, 128).transpose(2, 0, 1, 3).reshape(128, -1)
    out["lnp"] = np.stack([a["L1_ffn_ln_g"], a["L1_ffn_ln_b"]], -1).transpose(1, 0, 2).reshape(128, -1)
    out["b2"] = a["L1_ffn_b2"].T
    w1 = np.zeros((LAYERS, 128, 2, FCH * FW), np.float32)
    w1[..., :FI] = a["L1_ffn_W1"].reshape(LAYERS, 128, 2, FI)
    out["w1"] = w1.transpose(1, 0, 2, 3).reshape(128, -1)
    b1 = np.zeros((LAYERS, 2, FCH * FW), np.float32)
    b1[..., :FI] = a["L1_ffn_b1"].reshape(LAYERS, 2, FI)
    b1p = np.zeros((128, LAYERS * 2 * FCH), np.float32)
    b1p[:FW] = b1.reshape(LAYERS * 2 * FCH, FW).T
    out["b1"] = b1p
    w2 = np.zeros((LAYERS, FCH * FW, 128), np.float32)
    w2[:, :FI] = a["L1_ffn_W2"]
    out["w2"] = w2.reshape(LAYERS, FCH, FW, 128).transpose(2, 0, 1, 3).reshape(FW, -1)
    out.update(shape_constants())
    return {k: np.ascontiguousarray(v) for k, v in out.items()}


def kernel(**inputs):
    import concourse.bacc as bacc
    from concourse.bass_utils import run_bass_kernel_spmd

    arrays = layouts({k: np.asarray(v) for k, v in inputs.items()})
    nc = bacc.Bacc("TRN2", target_bir_lowering=False, num_devices=1)
    io = {k: nc.dram_tensor(f"in_{k}", v.shape, mybir.dt.from_np(v.dtype), kind="ExternalInput").ap()
          for k, v in arrays.items()}
    io["out"] = nc.dram_tensor("out_x", (128, TOK), F32, kind="ExternalOutput").ap()
    program(nc, io)
    r = run_bass_kernel_spmd(nc, [{f"in_{k}": v for k, v in arrays.items()}], core_ids=[0])
    return r.results[0]["out_x"].reshape(128, B, T).transpose(1, 2, 0)
```

```python
import numpy as np
from contextlib import ExitStack
import concourse.bass as bass
from concourse import mybir

F32 = mybir.dt.float32
BF16 = mybir.dt.bfloat16
U32 = mybir.dt.uint32
ALU = mybir.AluOpType
ACT = mybir.ActivationFunctionType
AX = mybir.AxisListType

B, T, D = 8, 256, 128
TOK = B * T
E, EH = 8, 256
CH = 512
NCH = TOK // CH
STEPS_CH = CH // B
HALVES = EH // 128
LAYERS, HEADS, HD, WIN = 6, 16, 64, 32
GROUPS, GH = 4, 4
QK = 2 * GH * HD
VC = GH * HD
GC = QK + VC
TILES = T // 128
FI = 341
FCH, FW = 3, 114
ALPHA_LO, ALPHA_HI = float(np.exp(-1.0 / 5.0)), float(np.exp(-1.0 / 25.0))
RS = 256.0
GS = 8
UNR = 16


def spiking_and_experts(nc, io, x1, lstm_xw):
    ctx = ExitStack()
    with ctx:
        def sb(name, shape, dt=F32):
            return ctx.enter_context(nc.sbuf_tensor(name, shape, dt))

        def pb(name, shape, dt=F32):
            return ctx.enter_context(nc.psum_tensor(name, shape, dt))

        def sem(name):
            return ctx.enter_context(nc.semaphore(name))

        xT = sb("xT", [128, TOK])
        condT = sb("condT", [128, B])
        wlif = sb("wlif", [128, 128])
        vlif = sb("vlif", [128, 128])
        al_col = sb("al_col", [128, 1])
        al_row = sb("al_row", [128, 128])
        ident = sb("ident", [128, 128])
        off_diag = sb("off_diag", [128, 128])
        iota = sb("iota", [128, E])
        wg = sb("wg", [128, E])
        w1 = sb("w1", [128, E * EH])
        b1 = sb("b1", [128, E * HALVES])
        w2 = sb("w2", [128, E * HALVES * 128])
        b2 = sb("b2", [E, 128])
        wx = sb("wx", [128, 4 * 128])
        bx = sb("bx", [128, 4])

        oma = sb("oma", [128, 1])
        noma = sb("noma", [128, 1])
        keep = sb("keep", [128, 128])
        vmat = sb("vmat", [128, 128])
        diag = sb("diag", [128, 128])
        vparts = sb("vparts", [128, 3, 128], BF16)
        vrest = sb("vrest", [128, 128])
        drive = sb("drive", [128, TOK + GS * B])
        spikes = sb("spikes", [128, TOK], BF16)
        margin = sb("margin", [128, 2, B])
        spk = sb("spk", [128, 2 * GS, B], BF16)
        w1p = sb("w1p", [128, 3, E * EH], BF16)
        w1r = sb("w1r", [128, E * EH])
        wgp = sb("wgp", [128, 3, E], BF16)
        wgr = sb("wgr", [128, E])

        chunk = sb("chunk", [128, CH], BF16)
        lmax = sb("lmax", [128, 4])
        lsub = sb("lsub", [128, 4, E])
        lexp = sb("lexp", [128, 4, E])
        lsum = sb("lsum", [128, 4])
        spare = sb("spare", [128, 1])
        probs = sb("probs", [128, 4, E])
        top = sb("top", [128, 4, 8])
        topi = sb("topi", [128, 4, 8], U32)
        topf = sb("topf", [128, 4, 8])
        pick = sb("pick", [128, 2, 4, E])
        gate = sb("gate", [128, 4, E])
        gateT = sb("gateT", [E, 4, 128])
        hid = sb("hid", [128, 2, HALVES, CH])
        acc = sb("acc", [128, 4, 128])
        x1c = sb("x1c", [128, CH])

        p_h = [pb(f"p_h{i}", [128, CH]) for i in range(2)]
        p_y = [pb(f"p_y{i}", [128, CH]) for i in range(2)]
        p_g = pb("p_g", [128, 512])
        p_t = pb("p_t", [128, 512])
        p_r = [pb(f"p_r{i}", [128, 512]) for i in range(2)]
        p_rec = [p_r, [p_g, p_t]]

        def product(j):
            return p_rec[j // GS][j % 2][:, j % GS // 2 * B:(j % GS // 2 + 1) * B]

        in_lif, in_moe = sem("in_lif"), sem("in_moe")
        vready, wx_mm, drive_ok = sem("vready"), sem("wx_mm"), sem("drive_ok")
        prep, moe_prep = sem("prep"), sem("moe_prep")
        rec_mm, spike_ok, margin_ok, hist_ok, first_ok = (
            sem("rec_mm"), sem("spike_ok"), sem("margin_ok"), sem("hist_ok"), sem("first_ok"))
        chunk_ok, logit_mm, lsub_ok, lexp_ok, gch = (
            sem("chunk_ok"), sem("logit_mm"), sem("lsub_ok"), sem("lexp_ok"), sem("gch"))
        gate_ok, gateT_mm, gateT_ok = sem("gate_ok"), sem("gateT_mm"), sem("gateT_ok")
        h_mm, h_ok, y_mm, acc_ok = sem("h_mm"), sem("h_ok"), sem("y_mm"), sem("acc_ok")
        out_mm, x1_ok, xw_mm, xw_ok = sem("out_mm"), sem("x1_ok"), sem("xw_mm"), sem("xw_ok")

        block = ctx.enter_context(nc.Block())

        @block.sync
        def _(sp):
            for dst, name in ((al_col, "alpha_col"), (wlif, "wlif"), (vlif, "vlif"), (ident, "ident"),
                              (off_diag, "off_diag"), (condT, "condT"), (xT, "xT")):
                sp.dma_start(dst[:], io[name]).then_inc(in_lif, 16)
            sp.dma_start(al_row[:], io["alpha_row"].partition_broadcast(128)).then_inc(in_lif, 16)
            for dst, name in ((w1, "e_w1"), (wg, "wg"), (iota, "iota"), (b1, "e_b1"), (w2, "e_w2"),
                              (b2, "e_b2"), (wx, "wx"), (bx, "bx")):
                sp.dma_start(dst[:], io[name]).then_inc(in_moe, 16)

        @block.tensor
        def _(pe):
            pe.wait_ge(in_lif, 128)
            for c in range(NCH):
                if c >= 2:
                    pe.wait_ge(drive_ok, c - 1)
                pe.matmul(p_h[c % 2][:], wlif[:], xT[:, c * CH:(c + 1) * CH], start=True, stop=True).then_inc(wx_mm, 1)
            def seed(t, banks):
                of_group = drive[:, bass.ds(t * B, GS * B)].rearrange("p (k two b) -> p two k b", two=2, b=B)
                for par in range(2):
                    pe.matmul(banks[par][:, 0:GS // 2 * B], ident[:], of_group[:, par], start=True, stop=False,
                              skip_group_check=True)

            def step(t, j):
                pe.wait_ge(spike_ok, t)
                for k in range(3):
                    last = pe.matmul(product(j), vparts[:, k, :], spk[:, (j - 1) % (2 * GS), :],
                                     start=False, stop=(k == 2), skip_group_check=True)
                last.then_inc(rec_mm, 1)

            def two_groups(t0, first):
                for j in range(2 * GS):
                    if j % GS == GS // 2:
                        if not first or j > GS:
                            pe.wait_ge(hist_ok, (t0 // GS if first else t0 >> 3) + j // GS)
                        seed(t0 + j + GS // 2, p_rec[1 - j // GS])
                    if first and j == 0:
                        pe.matmul(product(0), vmat[:], condT[:], start=False, stop=True,
                                  skip_group_check=True).then_inc(rec_mm, 1)
                    else:
                        step(t0 + j, j)

            pe.wait_ge(vready, 1)
            pe.wait_ge(drive_ok, NCH + 1)
            seed(0, p_rec[0])
            two_groups(0, True)
            with pe.Fori(1, T // (2 * GS)) as i:
                two_groups(i * (2 * GS), False)

            with pe.Fori(0, NCH) as c:
                pe.wait_ge(chunk_ok, c + 1)
                for j in range(4):
                    for k in range(3):
                        last = pe.matmul(p_g[:, j * E:(j + 1) * E], chunk[:, j * 128:(j + 1) * 128], wgp[:, k, :],
                                         start=(k == 0), stop=(k == 2))
                last.then_inc(logit_mm, 1)

                def up(e):
                    for h in range(HALVES):
                        n = e * HALVES + h
                        if n >= 2:
                            pe.wait_ge(h_ok, c * (E * HALVES) + n - 1)
                        for k in range(3):
                            last = pe.matmul(p_h[n % 2][:], w1p[:, k, e * EH + h * 128:e * EH + (h + 1) * 128],
                                             chunk[:], start=(k == 0), stop=(k == 2))
                        last.then_inc(h_mm, 1)

                def down(e):
                    pe.wait_ge(h_ok, c * (E * HALVES) + e * HALVES + HALVES)
                    if e >= 2:
                        pe.wait_ge(acc_ok, c * E + e - 1)
                    for j in range(4):
                        for h in range(HALVES):
                            last = pe.matmul(p_y[e % 2][:, j * 128:(j + 1) * 128], hid[:, e % 2, h, j * 128:(j + 1) * 128],
                                             w2[:, (e * HALVES + h) * 128:(e * HALVES + h + 1) * 128],
                                             start=(h == 0), stop=(h == HALVES - 1))
                    last.then_inc(y_mm, 1)

                up(0)
                for e in range(E):
                    if e + 1 < E:
                        up(e + 1)
                    down(e)
                pe.wait_ge(gate_ok, c + 1)
                for j in range(4):
                    last = pe.transpose(p_g[0:E, j * 128:(j + 1) * 128], gate[:, j, :], ident[:])
                last.then_inc(gateT_mm, 1)
                pe.wait_ge(acc_ok, c * E + E)
                pe.wait_ge(gateT_ok, c + 1)
                for j in range(4):
                    pe.matmul(p_t[:, j * 128:(j + 1) * 128], acc[:, j, :], ident[:], start=True, stop=False)
                    last = pe.matmul(p_t[:, j * 128:(j + 1) * 128], b2[:], gateT[:, j, :], start=False, stop=True)
                last.then_inc(out_mm, 1)
                pe.wait_ge(x1_ok, c + 1)
                for g in range(4):
                    if g >= 2:
                        pe.wait_ge(xw_ok, c * 4 + g - 1)
                    pe.matmul(p_h[g % 2][:], wx[:, g * 128:(g + 1) * 128], x1c[:], start=True, stop=True).then_inc(xw_mm, 1)
                pe.wait_ge(xw_ok, c * 4 + 4)

        @block.scalar
        def _(act):
            with act.Fori(0, NCH) as c:
                for n in range(E * HALVES):
                    act.wait_ge(h_mm, c * (E * HALVES) + n + 1)
                    e, h = divmod(n, HALVES)
                    if e >= 2:
                        act.wait_ge(y_mm, c * E + e - 1)
                    act.activation(hid[:, e % 2, h, :], p_h[n % 2][:], ACT.Relu, bias=b1[:, n:n + 1]).then_inc(h_ok, 1)
                    if n == 1:
                        act.wait_ge(lsub_ok, c + 1)
                        act.activation(lexp[:], lsub[:], ACT.Exp).then_inc(lexp_ok, 1)
                act.wait_ge(gateT_mm, c + 1)
                act.activation(gateT[:].rearrange("e j p -> e (j p)"), p_g[0:E, :], ACT.Copy).then_inc(gateT_ok, 1)
                for g in range(4):
                    act.wait_ge(xw_mm, c * 4 + g + 1)
                    dst = lstm_xw[:, bass.ds(c * (STEPS_CH * 4 * B), STEPS_CH * 4 * B)].rearrange(
                        "p (t g b) -> p t g b", g=4, b=B)[:, :, g, :]
                    act.activation(dst, p_h[g % 2][:].rearrange("p (t b) -> p t b", b=B), ACT.Identity,
                                   bias=bx[:, g:g + 1], scale=0.5 if g < 3 else 1.0).then_inc(xw_ok, 1)

        @block.gpsimd
        def _(pool):
            with pool.Fori(0, T // (2 * GS)) as i:
                for half in range(2):
                    pool.wait_ge(spike_ok, i * (2 * GS) + (half + 1) * GS)
                    pool.tensor_copy(spikes[:, bass.ds(i * (2 * GS * B) + half * (GS * B), GS * B)],
                                     spk[:, half * GS:(half + 1) * GS, :].rearrange("p t b -> p (t b)")).then_inc(hist_ok, 1)

        @block.vector
        def _(dve):
            done = [0]

            def link(ins):
                done[0] += 1
                ins.then_inc(prep, 1)
                dve.wait_ge(prep, done[0])

            dve.wait_ge(in_lif, 128)
            link(dve.tensor_scalar(al_col[:], al_col[:], ALPHA_LO, ALPHA_HI, ALU.max, ALU.min))
            dve.tensor_scalar(al_row[:], al_row[:], ALPHA_LO, ALPHA_HI, ALU.max, ALU.min)
            dve.tensor_scalar(oma[:], al_col[:], -1.0, 1.0, ALU.mult, ALU.add)
            link(dve.tensor_scalar(noma[:], al_col[:], 1.0, -1.0, ALU.mult, ALU.add))
            link(dve.tensor_scalar(keep[:], al_row[:], -1.0, 1.0, ALU.mult, ALU.add))
            link(dve.tensor_tensor(keep[:], keep[:], off_diag[:], ALU.mult))
            dve.tensor_tensor(vmat[:], vlif[:], keep[:], ALU.mult)
            link(dve.tensor_tensor(diag[:], al_row[:], ident[:], ALU.mult))
            link(dve.tensor_tensor(vmat[:], vmat[:], diag[:], ALU.subtract))
            dve.nop().then_inc(vready, 1)

            def split(parts, src, rest):
                link(dve.tensor_copy(parts(0), src))
                link(dve.tensor_tensor(rest, src, parts(0), ALU.subtract))
                link(dve.tensor_copy(parts(1), rest))
                link(dve.tensor_tensor(rest, rest, parts(1), ALU.subtract))
                link(dve.tensor_copy(parts(2), rest))

            split(lambda k: vparts[:, k, :], vmat[:], vrest[:])
            for c in range(NCH):
                dve.wait_ge(wx_mm, c + 1)
                ins = dve.tensor_scalar(drive[:, c * CH:(c + 1) * CH], p_h[c % 2][:], oma[:], noma[:], ALU.mult, ALU.add)
                ins.then_inc(drive_ok, 1)
            dve.memset(drive[:, TOK:TOK + GS * B], 0.0).then_inc(drive_ok, 1)
            dve.wait_ge(drive_ok, NCH + 1)
            dve.tensor_scalar(margin[:, 1, :], condT[:], -1.0, 1.0, ALU.mult, ALU.add).then_inc(first_ok, 1)
            dve.wait_ge(first_ok, 1)

            def step(t, j, first=False):
                m_before, m = margin[:, (j + 1) % 2, :], margin[:, j % 2, :]
                if not first:
                    dve.wait_ge(margin_ok, t)
                dve.wait_ge(rec_mm, t + 1)
                dve.scalar_tensor_tensor(spk[:, j, :], m_before, al_col[:], product(j),
                                         ALU.mult, ALU.is_lt).then_inc(spike_ok, 1)
                dve.scalar_tensor_tensor(m, m_before, al_col[:], product(j),
                                         ALU.mult, ALU.subtract).then_inc(margin_ok, 1)

            for t in range(2 * GS):
                step(t, t, t == 0)
            with dve.Fori(1, T // (2 * GS)) as i:
                t0 = i * (2 * GS)
                for j in range(2 * GS):
                    step(t0 + j, j)

            dve.wait_ge(in_moe, 128)
            dve.tensor_scalar(bx[:, 0:3], bx[:, 0:3], 0.5, None, ALU.mult)
            split(lambda k: wgp[:, k, :], wg[:], wgr[:])
            split(lambda k: w1p[:, k, :], w1[:], w1r[:])
            dve.wait_ge(hist_ok, T // GS)
            with dve.Fori(0, NCH) as c:
                dve.tensor_copy(chunk[:], spikes[:, bass.ds(c * CH, CH)]).then_inc(chunk_ok, 1)
                dve.wait_ge(logit_mm, c + 1)
                LINKS = 9
                k = [0]

                def link_c(ins):
                    k[0] += 1
                    ins.then_inc(gch, 1)
                    dve.wait_ge(gch, c * LINKS + k[0])

                lg = p_g[:, 0:4 * E].rearrange("p (j e) -> p j e", e=E)
                link_c(dve.tensor_reduce(lmax[:], lg, AX.X, ALU.max))
                dve.tensor_tensor(lsub[:], lg, lmax[:].unsqueeze(2).broadcast_to([128, 4, E]), ALU.subtract).then_inc(lsub_ok, 1)
                dve.wait_ge(lexp_ok, c + 1)
                link_c(dve.tensor_reduce(lsum[:], lexp[:], AX.X, ALU.add))
                link_c(dve.reciprocal(lsum[:], lsum[:]))
                link_c(dve.tensor_tensor(probs[:], lexp[:], lsum[:].unsqueeze(2).broadcast_to([128, 4, E]), ALU.mult))
                dve.tensor_copy(spare[:], lsum[:, 0:1])
                for j in range(4):
                    ins = dve.max(top[:, j, :], probs[:, j, :])
                link_c(ins)
                dve.tensor_copy(spare[:], lsum[:, 0:1])
                for j in range(4):
                    ins = dve.max_index(topi[:, j, :], top[:, j, :], probs[:, j, :])
                link_c(ins)
                link_c(dve.tensor_copy(topf[:], topi[:]))
                for j in range(4):
                    for r in range(2):
                        ins = dve.tensor_scalar(pick[:, r, j, :], iota[:], topf[:, j, r:r + 1], top[:, j, r:r + 1],
                                                ALU.is_equal, ALU.mult)
                link_c(ins)
                dve.tensor_tensor(gate[:], pick[:, 0], pick[:, 1], ALU.add).then_inc(gate_ok, 1)
                dve.wait_ge(gate_ok, c + 1)
                for e in range(E):
                    dve.wait_ge(y_mm, c * E + e + 1)
                    if e:
                        dve.wait_ge(acc_ok, c * E + e)
                    for j in range(4):
                        y = p_y[e % 2][:, j * 128:(j + 1) * 128]
                        if e == 0:
                            ins = dve.tensor_scalar(acc[:, j, :], y, gate[:, j, e:e + 1], None, ALU.mult)
                        else:
                            ins = dve.scalar_tensor_tensor(acc[:, j, :], y, gate[:, j, e:e + 1], acc[:, j, :], ALU.mult, ALU.add)
                    ins.then_inc(acc_ok, 1)
                dve.wait_ge(out_mm, c + 1)
                dve.tensor_tensor(x1c[:], p_t[:], xT[:, bass.ds(c * CH, CH)], ALU.add).then_inc(x1_ok, 1)
                dve.wait_ge(x1_ok, c + 1)
                link_c(dve.tensor_copy(x1[:, bass.ds(c * CH, CH)], x1c[:]))
                dve.wait_ge(xw_mm, c * 4 + 4)


def lstm(nc, io, hs, lstm_xw):
    ctx = ExitStack()
    with ctx:
        def sb(name, shape, dt=F32):
            return ctx.enter_context(nc.sbuf_tensor(name, shape, dt))

        def sem(name):
            return ctx.enter_context(nc.semaphore(name))

        wh = sb("wh", [128, 512])
        whr = sb("whr", [128, 512])
        whp = sb("whp", [128, 3, 512], BF16)
        idn = sb("idn", [128, 128])
        h = sb("h", [128, 2, B])
        hr = sb("hr", [128, B])
        hp = sb("hp", [128, 3, B], BF16)
        half = sb("half", [128, 512])
        th = sb("th", [128, 4 * B])
        ig = sb("ig", [128, B])
        fc = sb("fc", [128, B])
        cell = sb("cell", [128, B])
        tc = sb("tc", [128, B])
        gates = [ctx.enter_context(nc.psum_tensor(f"gates{i}", [128, 512], F32)) for i in range(2)]

        in_h, wprep = sem("in_h"), sem("wprep")
        seed_mm, gates_mm = sem("seed_mm"), sem("gates_mm")
        th_ok, tc_ok = sem("th_ok"), sem("tc_ok")
        cell_ch, cell_ok, h_ch, h1_ok, h2_ok, h3_ok, hs_ok = (
            sem("cell_ch"), sem("cell_ok"), sem("h_ch"), sem("h1_ok"), sem("h2_ok"), sem("h3_ok"), sem("hs_ok"))
        hfull = sem("hfull")

        block = ctx.enter_context(nc.Block())

        @block.sync
        def _(sp):
            sp.dma_start(wh[:], io["wh"]).then_inc(in_h, 16)
            sp.dma_start(h[:, 1, :], io["condT"]).then_inc(in_h, 16)
            sp.dma_start(idn[:], io["ident"]).then_inc(in_h, 16)

        @block.tensor
        def _(pe):
            pe.wait_ge(in_h, 48)

            def step(t, bank, first):
                if not first:
                    pe.wait_ge(th_ok, t - 1)
                pe.matmul(gates[bank][:, 0:4 * B], idn[:], lstm_xw[:, bass.ds(t * 4 * B, 4 * B)], start=True, stop=False)
                for ready, k, parts in ((h1_ok, 0, (0, 1, 2)), (h2_ok, 1, (0, 1)), (h3_ok, 2, (0,))):
                    pe.wait_ge(ready, t + 1)
                    for w in parts:
                        for g in range(4):
                            last = pe.matmul(gates[bank][:, g * B:(g + 1) * B], whp[:, w, g * 128:(g + 1) * 128], hp[:, k, :],
                                             start=False, stop=(k == 2 and g == 3))
                last.then_inc(gates_mm, 1)

            for t in range(2):
                step(t, t % 2, True)
            for t in range(2, UNR):
                step(t, t % 2, False)
            with pe.Fori(1, T // UNR) as i:
                t0 = i * UNR
                for j in range(UNR):
                    step(t0 + j, j % 2, False)

        @block.scalar
        def _(act):
            def step(t, bank, first):
                act.wait_ge(gates_mm, t + 1)
                act.activation(th[:], gates[bank][:, 0:4 * B], ACT.Tanh).then_inc(th_ok, 1)
                act.wait_ge(cell_ok, t + 1)
                act.activation(tc[:], cell[:], ACT.Tanh, scale=0.5).then_inc(tc_ok, 1)

            act.preload_act_table_set("sigmoid_and_others")
            with act.Fori(0, T // UNR) as i:
                t0 = i * UNR
                for j in range(UNR):
                    step(t0 + j, j % 2, False)

        @block.vector
        def _(dve):
            done = [0]

            def link(ins):
                done[0] += 1
                ins.then_inc(wprep, 1)
                dve.wait_ge(wprep, done[0])

            dve.wait_ge(in_h, 48)
            link(dve.memset(cell[:], 0.0))
            dve.memset(half[:, 0:384], 0.5)
            link(dve.memset(half[:, 384:512], 1.0))
            link(dve.scalar_tensor_tensor(wh[:], wh[:], 0.5, half[:], ALU.mult, ALU.mult))
            link(dve.tensor_scalar(h[:, 1, :], h[:, 1, :], 2.0, None, ALU.mult))
            link(dve.tensor_copy(whp[:, 0, :], wh[:]))
            link(dve.tensor_tensor(whr[:], wh[:], whp[:, 0, :], ALU.subtract))
            link(dve.tensor_copy(whp[:, 1, :], whr[:]))
            link(dve.tensor_tensor(whr[:], whr[:], whp[:, 1, :], ALU.subtract))
            link(dve.tensor_copy(whp[:, 2, :], whr[:]))
            link(dve.tensor_copy(hp[:, 0, :], h[:, 1, :]))
            dve.nop().then_inc(h1_ok, 1)
            link(dve.tensor_tensor(hr[:], h[:, 1, :], hp[:, 0, :], ALU.subtract))
            link(dve.tensor_copy(hp[:, 1, :], hr[:]))
            dve.nop().then_inc(h2_ok, 1)
            link(dve.tensor_tensor(hp[:, 2, :], hr[:], hp[:, 1, :], ALU.subtract))
            dve.nop().then_inc(h3_ok, 1)

            def step(t, buf):
                dve.wait_ge(th_ok, t + 1)
                dve.scalar_tensor_tensor(fc[:], th[:, B:2 * B], 1.0, cell[:], ALU.add, ALU.mult)
                dve.scalar_tensor_tensor(ig[:], th[:, 0:B], 1.0, th[:, 3 * B:4 * B], ALU.add, ALU.mult).then_inc(cell_ch, 1)
                dve.wait_ge(cell_ch, t + 1)
                dve.scalar_tensor_tensor(cell[:], fc[:], 0.5, ig[:], ALU.mult, ALU.add).then_inc(cell_ok, 1)
                dve.wait_ge(tc_ok, t + 1)
                o = th[:, 2 * B:3 * B]
                dve.scalar_tensor_tensor(hp[:, 0, :], o, 1.0, tc[:], ALU.add, ALU.mult).then_inc(h1_ok, 1)
                dve.scalar_tensor_tensor(h[:, buf, :], o, 1.0, tc[:], ALU.add, ALU.mult).then_inc(hfull, 1)
                dve.wait_ge(hfull, t + 1)
                dve.tensor_tensor(hp[:, 1, :], h[:, buf, :], hp[:, 0, :], ALU.subtract).then_inc(h2_ok, 1)
                dve.tensor_tensor(hr[:], h[:, buf, :], hp[:, 0, :], ALU.subtract).then_inc(h_ch, 1)
                dve.wait_ge(h_ch, t + 1)
                dve.tensor_tensor(hp[:, 2, :], hr[:], hp[:, 1, :], ALU.subtract).then_inc(h3_ok, 1)

            with dve.Fori(0, T // UNR) as i:
                t0 = i * UNR
                for j in range(UNR):
                    step(t0 + j, j % 2)
                    dve.wait_ge(hs_ok, t0 + j + 1)
            dve.tensor_scalar(hs[:], hs[:], 0.5, None, ALU.mult)

        @block.gpsimd
        def _(pool):
            hs_bt = hs[:].rearrange("p (b t) -> p b t", t=T)
            with pool.Fori(0, T // UNR) as i:
                t0 = i * UNR
                for j in range(UNR):
                    pool.wait_ge(hfull, t0 + j + 1)
                    pool.tensor_copy(hs_bt[:, :, bass.ds(t0 + j, 1)], h[:, j % 2, :].unsqueeze(2)).then_inc(hs_ok, 1)


def transformer(nc, io, x, x1):
    ctx = ExitStack()
    with ctx:
        def sb(name, shape, dt=F32):
            return ctx.enter_context(nc.sbuf_tensor(name, shape, dt))

        def sem(name):
            return ctx.enter_context(nc.semaphore(name))

        NS = LAYERS * B

        ident = sb("t_ident", [128, 128])
        identb = sb("t_identb", [128, 128], BF16)
        maskf = sb("t_maskf", [128, TILES * 2 * 2 * WIN])
        ones = sb("t_ones", [128, 128])
        mask = sb("t_mask", [128, TILES * 2 * 2 * WIN], BF16)
        rot = sb("t_rot", [128, TILES, 2, 2, HD])
        scl = sb("t_scl", [128, LAYERS, 2, 2, HD])
        tab = sb("t_tab", [128, LAYERS * TILES * 2 * 2 * HD])
        wqkv = sb("t_wqkv", [128, 2 * GROUPS * GC])
        wo = sb("t_wo", [128, 8, 128])
        w1 = sb("t_w1", [128, 2 * FCH, FW])
        b1 = sb("t_b1", [128, 2 * FCH])
        w2 = sb("t_w2", [FW, FCH, 128])
        b2 = sb("t_b2", [128, 1])
        lnp = sb("t_lnp", [128, 2])
        ln_bias = sb("t_eps", [128, 1])

        xs = sb("t_xs", [128, T])
        sq = sb("t_sq", [128, TILES, QK])
        ss = sb("t_ss", [128, TILES, 2 * GH])
        lns = sb("t_lns", [128, TILES, 2 * GH])
        ers = sb("t_ers", [128, TILES, 2 * GH])
        nt = sb("t_nt", [128, TILES, 2 * GH])
        rn = sb("t_rn", [128, TILES, 2 * GH])
        cosp = sb("t_cosp", [128, TILES, QK])
        sinp = sb("t_sinp", [128, TILES, QK])
        qkn = sb("t_qkn", [128, TILES, QK])
        vn = sb("t_vn", [128, GROUPS, TILES, VC])
        vp = sb("t_vp", [128, GROUPS, TILES, VC])
        qT = sb("t_qT", [128, 2, T])
        kT = sb("t_kT", [128, 2, WIN + T])
        smax = sb("t_smax", [128, 2, TILES, 2])
        ssub = sb("t_ssub", [128, 2, TILES, 2, 2 * WIN])
        prob = sb("t_prob", [128, 2, TILES, 2, 2 * WIN])
        psm = sb("t_psm", [128, 2, TILES, 2])
        pinv = sb("t_pinv", [128, 2, TILES, 2])
        cT = sb("t_cT", [128, 16, WIN])
        pT = sb("t_pT", [128, 2, 16, 128])
        oT = sb("t_oT", [128, 2, T])

        xf = sb("t_xf", [128, T])
        xc = sb("t_xc", [128, T])
        xq = sb("t_xq", [128, T])
        var = sb("t_var", [128, T])
        lnv = sb("t_lnv", [128, T])
        erv = sb("t_erv", [128, T])
        nv = sb("t_nv", [128, T])
        xh = sb("t_xh", [128, T])
        xn = sb("t_xn", [128, T])
        fa = sb("t_fa", [FW, FCH, T])
        fg = sb("t_fg", [FW, FCH, T])
        fh = sb("t_fh", [FW, FCH, T])

        def bank(name):
            return ctx.enter_context(nc.psum_tensor(name, [128, 512], F32))

        p_qk = [bank("p_qk0"), bank("p_qk1")]
        p_v, p_a, p_b, p_o = bank("p_v"), bank("p_a"), bank("p_b"), bank("p_o")
        p_s = [bank("p_s0"), bank("p_s1")]

        in_c, in_w = sem("in_c"), sem("in_w")
        in_wo, in_ln, in_w1, in_w2 = sem("in_wo"), sem("in_ln"), sem("in_w1"), sem("in_w2")
        tab_ch, tab_ok, zero_ok = sem("tab_ch"), sem("tab_ok"), sem("zero_ok")
        xs_ok, qk_mm, v_mm, sq_ok, v_ok = sem("xs_ok"), sem("qk_mm"), sem("v_mm"), sem("sq_ok"), sem("v_ok")
        vp_ok = [sem(f"vp_ok{g}") for g in range(GROUPS)]
        rot_ok, ss_ok, ln_ok, er_ok, n_ch, rn_ok = (
            sem("rot_ok"), sem("ss_ok"), sem("ln_ok"), sem("er_ok"), sem("n_ch"), sem("rn_ok"))
        add_ok, qkn_ok = sem("add_ok"), sem("qkn_ok")
        qT_mm, kT_mm, qT_ok, kT_ok = sem("qT_mm"), sem("kT_mm"), sem("qT_ok"), sem("kT_ok")
        s_mm, mx_ch, sub_ok, exp_ok, inv_ch, inv_ok, prob_ok, cT_ok, pT_ok = (
            sem("s_mm"), sem("mx_ch"), sem("sub_ok"), sem("exp_ok"), sem("inv_ch"), sem("inv_ok"), sem("prob_ok"),
            sem("cT_ok"), sem("pT_ok"))
        pv_mm, oT_ok, wo_mm, x_ok = sem("pv_mm"), sem("oT_ok"), sem("wo_mm"), sem("x_ok")
        xf_ok, mu_mm, xc_ok, xq_ok, var_mm = sem("xf_ok"), sem("mu_mm"), sem("xc_ok"), sem("xq_ok"), sem("var_mm")
        var_ok, lnv_ok, erv_ok, nv_ch, xh_ok, xn_ok = (
            sem("var_ok"), sem("lnv_ok"), sem("erv_ok"), sem("nv_ch"), sem("xh_ok"), sem("xn_ok"))
        up_mm, up_ok, gelu_ok, fh_ok, down_mm, ffn_ok = (
            sem("up_mm"), sem("up_ok"), sem("gelu_ok"), sem("fh_ok"), sem("down_mm"), sem("ffn_ok"))
        out_ok, stored = sem("out_ok"), sem("stored")

        block = ctx.enter_context(nc.Block())

        def whole(n):
            return isinstance(n, int)

        def live(n):
            return not whole(n) or 0 <= n < NS

        def has(n, g, back):
            return not whole(n) or 0 <= 4 * n + g - back < 4 * NS

        def loads(n, back):
            return (n - back) // B + 1 if whole(n) else (n + (B - back)) >> 3

        def layer(n):
            if whole(n):
                return n // B
            return nc.s_assert_within(n >> 3, 0, LAYERS - 1, skip_runtime_bounds_check_because="n is below LAYERS * B")

        def schedule(eng, unit):
            for n in range(3):
                for g in range(GROUPS):
                    unit(n, g)
            with eng.Fori(3, NS) as n:
                for g in range(GROUPS):
                    unit(n, g)
            for n in range(NS, NS + 3):
                for g in range(GROUPS):
                    unit(n, g)

        def seq(n, p0, p1, t0, t1):
            off = (n % B if whole(n) else n & (B - 1)) * T + t0
            return x[p0:p1, bass.ds(off, t1 - t0)]


        @block.sync
        def _(sp):
            for dst, name in ((ident, "ident"), (ones, "ones"), (maskf, "mask"), (rot, "rot")):
                sp.dma_start(dst[:], io[name]).then_inc(in_c, 16)
            for k, name in ((0, "q_scale"), (1, "k_scale")):
                s = io[name]
                sp.dma_start(scl[:, :, 0, k, :], s.partition_broadcast(128)).then_inc(in_c, 16)
                sp.dma_start(scl[:, :, 1, k, 0:32], s[:, 32:64].partition_broadcast(128)).then_inc(in_c, 16)
                sp.dma_start(scl[:, :, 1, k, 32:64], s[:, 0:32].partition_broadcast(128)).then_inc(in_c, 16)
            W = GROUPS * GC
            sp.dma_start(wqkv[:, 0:W], io["wqkv"][:, 0:W]).then_inc(in_w, 16)
            small = [(in_wo, wo, "wo"), (in_ln, lnp, "lnp"), (in_w1, w1, "w1"),
                     (in_w1, b1, "b1"), (in_w2, w2, "w2"), (in_w2, b2, "b2")]

            def width(name):
                return io[name].shape[1] // LAYERS

            def load(at, which):
                for s, dst, name in small:
                    if s is which:
                        flat = dst[:] if len(dst.shape) == 2 else dst[:].rearrange("p a b -> p (a b)")
                        sp.dma_start(flat, io[name][:, bass.ds(at[name], width(name))],
                                     allow_slow_non_contiguous=width(name) == 1).then_inc(s, 16)

            for s in (in_wo, in_ln, in_w1, in_w2):
                load({name: 0 for _, _, name in small}, s)
            sp.wait_ge(in_w, 16)
            sp.dma_start(wqkv[:, W:2 * W], io["wqkv"][:, W:2 * W]).then_inc(in_w, 16)

            def shift_v(n, g):
                sp.wait_ge(v_ok, 4 * n + g + 1)
                sp.dma_start(vp[WIN:128, g, :, :], vn[0:128 - WIN, g, :, :]).then_inc(vp_ok[g], 16)
                sp.dma_start(vp[0:WIN, g, 1:TILES, :], vn[128 - WIN:128, g, 0:TILES - 1, :]).then_inc(vp_ok[g], 16)

            with sp.Fori(0, B) as b:
                for g in range(GROUPS):
                    shift_v(b, g)
            for l in range(1, LAYERS):
                first = l * B
                at = {name: l * width(name) for _, _, name in small}
                for g in range(GROUPS):
                    shift_v(first, g)
                    if g == 2:
                        sp.wait_ge(wo_mm, 4 * first)
                        load(at, in_wo)
                        if l + 1 < LAYERS:
                            sp.wait_ge(v_mm, 4 * first)
                            slot = (l + 1) % 2 * W
                            sp.dma_start(wqkv[:, slot:slot + W], io["wqkv"][:, (l + 1) * W:(l + 2) * W]).then_inc(in_w, 16)
                for g in range(GROUPS):
                    shift_v(first + 1, g)
                    if g == 2:
                        sp.wait_ge(xn_ok, first)
                        load(at, in_ln)
                    if g == 3:
                        sp.wait_ge(up_ok, first * FCH)
                        load(at, in_w1)
                for g in range(GROUPS):
                    shift_v(first + 2, g)
                    if g == 1:
                        sp.wait_ge(ffn_ok, first)
                        load(at, in_w2)
                with sp.Fori(first + 3, first + B) as n:
                    for g in range(GROUPS):
                        shift_v(n, g)
            sp.wait_ge(out_ok, 1)
            sp.dma_start(io["out"], x[:]).then_inc(stored, 16)
            sp.wait_ge(stored, 16)

        @block.tensor
        def _(pe):
            pe.wait_ge(in_c, 16 * 10)
            pe.wait_ge(zero_ok, 1)

            def project(n, g):
                if g == 0:
                    pe.wait_ge(xs_ok, n + 1)
                    pe.wait_ge(in_w, 16 * loads(n, 0))
                base = g * GC if whole(n) else ((n >> 3) & 1) * (GROUPS * GC) + g * GC
                before = has(n, g, 1)
                for j in range(TILES):
                    if before:
                        pe.wait_ge(rot_ok, (4 * n + g) * TILES + j - TILES + 1)
                    pe.matmul(p_qk[j][:], xs[:, j * 128:(j + 1) * 128], wqkv[:, bass.ds(base, QK)],
                              start=True, stop=True).then_inc(qk_mm, 1)
                if before:
                    pe.wait_ge(v_ok, 4 * n + g)
                    if g == 2 and live(n - 2):
                        pe.wait_ge(up_ok, FCH * (n - 2) + 1)
                    if g == 1 and live(n - 3):
                        pe.wait_ge(ffn_ok, n - 2)
                for j in range(TILES):
                    last = pe.matmul(p_v[:, j * VC:(j + 1) * VC], xs[:, j * 128:(j + 1) * 128],
                                     wqkv[:, bass.ds(base + QK, VC)], start=True, stop=True)
                last.then_inc(v_mm, 1)

            def turn(n, g):
                u = 4 * n + g - 1
                if has(n, g, 2):
                    pe.wait_ge(qT_ok, u)
                if has(n, g, 4):
                    pe.wait_ge(x_ok, u - 2)
                if g == 0 and live(n - 2):
                    pe.wait_ge(xc_ok, n - 1)
                if g == 1 and live(n - 2):
                    pe.wait_ge(var_ok, n - 1)
                if g == 2 and live(n - 2):
                    pe.wait_ge(up_ok, FCH * (n - 2) + 2)
                if g == 3 and live(n - 2):
                    pe.wait_ge(up_ok, FCH * (n - 2) + 3)
                pe.wait_ge(qkn_ok, (u + 1) * TILES)
                for c, bank_, s in ((0, p_a, qT_mm), (1, p_b, kT_mm)):
                    for hp in range(2):
                        for j in range(TILES):
                            at = c * VC + hp * 128
                            last = pe.transpose(bank_[:, hp * T + j * 128:hp * T + (j + 1) * 128],
                                                qkn[:, j, at:at + 128], ident[:])
                    last.then_inc(s, 1)

            def values(n, g):
                u = 4 * n + g - 3
                s = (g + 1) % GROUPS
                pe.wait_ge(pT_ok, u + 1)
                pe.wait_ge(vp_ok[s], 32 * n + 32 if g == 3 else 32 * n)
                if has(n, g, 4):
                    pe.wait_ge(oT_ok, u)
                for j in range(TILES):
                    for hp in range(2):
                        for half, v in ((0, vp), (1, vn)):
                            for par in range(2):
                                h = 2 * hp + par
                                i = 2 * ((par * TILES + j) * 2 + hp) + half
                                o = p_o[64 * par:64 * par + 64, hp * T + j * 128:hp * T + (j + 1) * 128]
                                last = pe.matmul(o, v[:, s, j, h * HD:(h + 1) * HD], pT[:, (g + 1) % 2, i, :],
                                                 start=(half == 0), stop=(half == 1), skip_group_check=True)
                last.then_inc(pv_mm, 1)

            def scores(n, g):
                u = 4 * n + g - 1
                pe.wait_ge(qT_ok, u + 1)
                pe.wait_ge(kT_ok, u + 1)
                if has(n, g, 2):
                    pe.wait_ge(sub_ok, u)
                for par in range(2):
                    rows = slice(64 * par, 64 * par + 64)
                    pe.matmul(p_s[par][:, 0:256], identb[:], mask[:], start=True, stop=False, skip_group_check=True)
                    for j in range(TILES):
                        for hp in range(2):
                            for w in range(4):
                                col = (j * 2 + hp) * 2 * WIN
                                t = j * 128 + w * WIN
                                last = pe.matmul(p_s[par][w * WIN:(w + 1) * WIN, col:col + 2 * WIN],
                                                 qT[rows, hp, t:t + WIN], kT[rows, hp, t:t + 2 * WIN],
                                                 start=False, stop=True, skip_group_check=True)
                last.then_inc(s_mm, 1)

            def out_proj(n, g):
                u = 4 * n + g - 3
                pe.wait_ge(in_wo, 16 * loads(n, 1 if g < 3 else 0))
                pe.wait_ge(oT_ok, u + 1)
                if has(n, g, 1):
                    pe.wait_ge(kT_ok, u + 3)
                else:
                    pe.wait_ge(x_ok, u)
                for hp in range(2):
                    last = pe.matmul(p_b[:, 0:T], wo[:, (2 * (g - 3) + hp) % 8, :], oT[:, hp, :],
                                     start=(hp == 0), stop=(hp == 1))
                last.then_inc(wo_mm, 1)

            def q_out(n, g):
                u = 4 * n + g
                pe.wait_ge(qT_ok, min(u, 4 * NS) if whole(n) else u)

            def v_out(n, g):
                u = 4 * n + g + 1
                pe.wait_ge(v_ok, min(u, 4 * NS) if whole(n) else u)

            def up(m, c, bank_):
                for k in range(2):
                    last = pe.matmul(bank_[0:FW, k * T:(k + 1) * T], w1[:, k * FCH + c, :], xn[:], start=True, stop=True)
                last.then_inc(up_mm, 1)

            def feed_forward(n, g):
                if g == 0 and live(n - 2):
                    pe.wait_ge(xq_ok, n - 1)
                    q_out(n, g)
                    pe.wait_ge(xc_ok, n - 1)
                    pe.matmul(p_a[:, 0:T], ones[:], xq[:], start=True, stop=True).then_inc(var_mm, 1)
                if g == 1 and live(n - 2):
                    pe.wait_ge(xn_ok, n - 1)
                    pe.wait_ge(in_w1, 32 * loads(n, 2))
                    v_out(n, g)
                    up(n - 2, 0, p_v)
                    q_out(n, g)
                    pe.wait_ge(var_ok, n - 1)
                    up(n - 2, 1, p_a)
                if g == 2 and live(n - 2):
                    q_out(n, g)
                    pe.wait_ge(up_ok, FCH * (n - 2) + 2)
                    up(n - 2, 2, p_a)

            def mean(n, g):
                if g == 3 and live(n - 1):
                    pe.wait_ge(xf_ok, n)
                    q_out(n, g)
                    if live(n - 2):
                        pe.wait_ge(up_ok, FCH * (n - 1))
                    pe.matmul(p_a[:, 0:T], ones[:], xf[:], start=True, stop=True).then_inc(mu_mm, 1)

            def down(n, g):
                if g == 0 and live(n - 3):
                    pe.wait_ge(fh_ok, n - 2)
                    pe.wait_ge(in_w2, 32 * loads(n, 3))
                    v_out(n, g)
                    for c in range(FCH):
                        last = pe.matmul(p_v[:, 0:T], w2[:, c, :], fh[:, c, :], start=(c == 0), stop=(c == FCH - 1))
                    last.then_inc(down_mm, 1)

            def unit(n, g):
                if has(n, g, 0):
                    project(n, g)
                if has(n, g, 1):
                    turn(n, g)
                if has(n, g, 3):
                    values(n, g)
                down(n, g)
                if has(n, g, 1):
                    scores(n, g)
                mean(n, g)
                if has(n, g, 3):
                    out_proj(n, g)
                feed_forward(n, g)

            schedule(pe, unit)

        @block.scalar
        def _(act):
            act.preload_act_table_set("natural_log_exp_and_others")
            act.wait_ge(zero_ok, 1)

            def copies_in(n, g):
                u = 4 * n + g
                for j in range(TILES):
                    act.wait_ge(qk_mm, u * TILES + j + 1)
                    if has(n, g, 1):
                        act.wait_ge(ss_ok, u)
                    act.activation(sq[:, j, :], p_qk[j][:], ACT.Square).then_inc(sq_ok, 1)
                act.wait_ge(v_mm, u + 1)
                if live(n - 1):
                    act.wait_ge(pv_mm, u - 3)
                act.activation(vn[:, g, :, :].rearrange("p j c -> p (j c)"), p_v[:], ACT.Copy).then_inc(v_ok, 1)

            def inverse_norms(n, g):
                u = 4 * n + g
                act.wait_ge(ss_ok, u + 1)
                act.activation(lns[:], ss[:], ACT.Ln, scale=RS * RS).then_inc(ln_ok, 1)
                act.wait_ge(ln_ok, u + 1)
                if has(n, g, 1):
                    act.wait_ge(rn_ok, u)
                act.activation(ers[:], lns[:], ACT.Exp, scale=-0.5).then_inc(er_ok, 1)

            def turned(n, g):
                u = 4 * n + g - 1
                act.wait_ge(qT_mm, u + 1)
                if has(n, g, 2):
                    act.wait_ge(s_mm, u)
                act.activation(qT[:].rearrange("p a t -> p (a t)"), p_a[:], ACT.Copy).then_inc(qT_ok, 1)
                act.wait_ge(kT_mm, u + 1)
                act.activation(kT[:, :, WIN:WIN + T], p_b[:].rearrange("p (a t) -> p a t", a=2), ACT.Copy).then_inc(kT_ok, 1)

            def exps(n, g):
                u = 4 * n + g - 1
                act.wait_ge(sub_ok, u + 1)
                if has(n, g, 2):
                    act.wait_ge(cT_ok, u)
                act.activation(prob[:], ssub[:], ACT.Exp).then_inc(exp_ok, 1)

            def spread(n, g, windows):
                u = 4 * n + g - 2
                if 0 in windows:
                    act.wait_ge(cT_ok, u + 1)
                    if has(n, g, 4):
                        act.wait_ge(pv_mm, u - 1)
                for w in windows:
                    rows = slice(w * WIN, (w + 1) * WIN)
                    ins = act.activation(pT[rows, g % 2, :, w * WIN:(w + 1) * WIN], cT[rows, :, :], ACT.Copy)
                if 3 in windows:
                    ins.then_inc(pT_ok, 1)

            def turned_out(n, g):
                u = 4 * n + g - 3
                act.wait_ge(pv_mm, u + 1)
                if has(n, g, 4):
                    act.wait_ge(wo_mm, u)
                act.activation(oT[:].rearrange("p a t -> p (a t)"), p_o[:], ACT.Copy).then_inc(oT_ok, 1)

            def up_out(n, g, at, c, bank_):
                if g == at and live(n - 2):
                    m = n - 2
                    if c == 0 and live(n - 3):
                        act.wait_ge(fh_ok, m)
                    act.wait_ge(up_mm, FCH * m + c + 1)
                    act.wait_ge(in_w1, 32 * loads(n, 2))
                    for k, dst in ((0, fa), (1, fg)):
                        ins = act.activation(dst[:, c, :], bank_[0:FW, k * T:(k + 1) * T], ACT.Identity,
                                             bias=b1[0:FW, k * FCH + c:k * FCH + c + 1])
                    ins.then_inc(up_ok, 1)

            def normalised(n, g):
                if g == 1 and live(n - 2):
                    m = n - 2
                    act.wait_ge(xh_ok, m + 1)
                    act.wait_ge(in_ln, 16 * loads(n, 2))
                    act.activation(xn[:], xh[:], ACT.Identity, bias=lnp[:, 1:2], scale=lnp[:, 0:1]).then_inc(xn_ok, 1)

            def feed_forward(n, g):
                if g == 3 and live(n - 1):
                    m = n - 1
                    act.wait_ge(x_ok, 4 * n)
                    if live(n - 2):
                        act.wait_ge(xc_ok, m)
                    act.activation(xf[0:64, :], seq(m, 0, 64, 0, T), ACT.Copy)
                    act.activation(xf[64:128, 1:T], seq(m, 64, 128, 0, T - 1), ACT.Copy).then_inc(xf_ok, 1)

            def variance(n, g):
                if g == 0 and live(n - 2):
                    m = n - 2
                    act.wait_ge(var_mm, m + 1)
                    act.activation(var[:], p_a[:, 0:T], ACT.Identity, bias=ln_bias[:]).then_inc(var_ok, 1)
                    act.wait_ge(var_ok, m + 1)
                    act.activation(lnv[:], var[:], ACT.Ln).then_inc(lnv_ok, 1)
                    act.wait_ge(lnv_ok, m + 1)
                    act.activation(erv[:], lnv[:], ACT.Exp, scale=-0.5).then_inc(erv_ok, 1)

            def gelu(n, g):
                if g == 3 and live(n - 2):
                    act.wait_ge(up_ok, FCH * (n - 1))
                    flat = fg[:].rearrange("p c t -> p (c t)")
                    act.activation(flat, flat, ACT.Gelu).then_inc(gelu_ok, 1)
                    act.preload_act_table_set("natural_log_exp_and_others")

            def unit(n, g):
                if has(n, g, 0):
                    copies_in(n, g)
                if has(n, g, 1):
                    turned(n, g)
                feed_forward(n, g)
                if has(n, g, 3):
                    turned_out(n, g)
                normalised(n, g)
                if has(n, g, 0):
                    inverse_norms(n, g)
                if has(n, g, 2):
                    spread(n, g, (0, 1, 2, 3))
                up_out(n, g, 1, 0, p_v)
                if has(n, g, 1):
                    exps(n, g)
                variance(n, g)
                up_out(n, g, 1, 1, p_a)
                up_out(n, g, 2, 2, p_a)
                gelu(n, g)

            schedule(act, unit)

        @block.vector
        def _(dve):
            dve.memset(vp[0:WIN, :, 0:1, :], 0.0)
            dve.memset(kT[:, :, 0:WIN], 0.0)
            dve.memset(pT[:], 0.0)
            dve.memset(xs[64:128, 0:1], 0.0)
            dve.memset(xf[64:128, 0:1], 0.0)
            dve.memset(ln_bias[:], 1e-5)
            dve.wait_ge(in_c, 16 * 10)
            dve.tensor_copy(identb[:], ident[:])
            dve.tensor_copy(mask[:], maskf[:]).then_inc(zero_ok, 1)
            dve.wait_ge(zero_ok, 1)

            def shift_in(n):
                dve.tensor_copy(xs[0:64, :], seq(n, 0, 64, 0, T))
                dve.tensor_copy(xs[64:128, 1:T], seq(n, 64, 128, 0, T - 1)).then_inc(xs_ok, 1)

            shift_in(0)
            dve.wait_ge(tab_ok, 1)

            def rotate(n, g):
                u = 4 * n + g
                lay = layer(n) * (TILES * 256)
                if has(n, g, 1):
                    dve.wait_ge(qkn_ok, u * TILES)
                for j in range(TILES):
                    dve.wait_ge(sq_ok, u * TILES + j + 1)
                    if j == 0 and has(n, g, 1):
                        dve.wait_ge(er_ok, u)
                    q = p_qk[j][:].rearrange("p (k h d) -> p k h d", k=2, h=GH)
                    c = cosp[:, j, :].rearrange("p (k h d) -> p k h d", k=2, h=GH)
                    s = sinp[:, j, :].rearrange("p (k h d) -> p k h d", k=2, h=GH)

                    def table(which, d0, d1):
                        t = tab[:, bass.ds(lay + j * 256 + which * 128, 128)].rearrange("p (k d) -> p k d", k=2)
                        return t[:, :, d0:d1].unsqueeze(2).broadcast_to([128, 2, GH, d1 - d0])

                    def squares():
                        return dve.tensor_reduce(ss[:, j, :], sq[:, j, :].rearrange("p (h d) -> p h d", d=HD), AX.X, ALU.add)

                    last = j == TILES - 1
                    ins = squares()
                    if last:
                        ins.then_inc(n_ch, 1)
                    inverse_deviation(n, g, 2 * j)
                    dve.tensor_tensor(c, q, table(0, 0, HD), ALU.mult)
                    if last:
                        dve.wait_ge(n_ch, 3 * u + 1)
                        dve.tensor_scalar(ss[:], ss[:], 1e-24, None, ALU.max).then_inc(ss_ok, 1)
                    inverse_deviation(n, g, 2 * j + 1)
                    dve.tensor_tensor(s[:, :, :, 0:32], q[:, :, :, 32:64], table(1, 0, 32), ALU.mult)
                    dve.tensor_tensor(s[:, :, :, 32:64], q[:, :, :, 0:32], table(1, 32, 64), ALU.mult).then_inc(rot_ok, 1)

            def norms(n, g):
                u = 4 * n + g
                dve.wait_ge(er_ok, u + 1)
                dve.scalar_tensor_tensor(nt[:], ers[:], RS * RS, ers[:], ALU.mult, ALU.mult).then_inc(n_ch, 1)
                dve.wait_ge(n_ch, 3 * u + 2)
                dve.scalar_tensor_tensor(nt[:], nt[:], -0.5, ss[:], ALU.mult, ALU.mult).then_inc(n_ch, 1)
                dve.wait_ge(n_ch, 3 * u + 3)
                dve.scalar_tensor_tensor(rn[:], nt[:], 1.5, ers[:], ALU.add, ALU.mult).then_inc(rn_ok, 1)

            def softmax(n, g):
                u = 4 * n + g - 1
                dve.wait_ge(s_mm, u + 1)
                s = [p_s[par][:, 0:256].rearrange("p (q c) -> p q c", c=2 * WIN) for par in range(2)]
                m = smax[:].rearrange("p a j b -> p a (j b)")
                for par in range(2):
                    ins = dve.tensor_reduce(m[:, par, :], s[par], AX.X, ALU.max)
                ins.then_inc(mx_ch, 1)
                dve.wait_ge(mx_ch, u + 1)
                if has(n, g, 2):
                    dve.wait_ge(exp_ok, u)
                z = ssub[:].rearrange("p a j b c -> p a (j b) c")
                for par in range(2):
                    ins = dve.tensor_tensor(z[:, par], s[par], m[:, par, :].unsqueeze(2).broadcast_to([128, 4, 2 * WIN]),
                                            ALU.subtract)
                ins.then_inc(sub_ok, 1)

            def sums(n, g):
                u = 4 * n + g - 1
                dve.wait_ge(exp_ok, u + 1)
                p = prob[:].rearrange("p a j b c -> p (a j b) c")
                dve.tensor_reduce(psm[:].rearrange("p a j b -> p (a j b)"), p, AX.X, ALU.add).then_inc(inv_ch, 1)
                dve.wait_ge(inv_ch, u + 1)
                dve.reciprocal(pinv[:], psm[:]).then_inc(inv_ok, 1)

            def turned_probs(n, g):
                u = 4 * n + g - 2
                dve.wait_ge(prob_ok, u + 1)
                if has(n, g, 3):
                    dve.wait_ge(pT_ok, u)
                dve.transpose(cT[:].rearrange("p i c -> p (i c)"), prob[:].rearrange("p a j b c -> p (a j b c)")).then_inc(cT_ok, 1)

            def residual(n, g):
                u = 4 * n + g - 3
                m = n - 1 if g < 3 else n
                dve.wait_ge(wo_mm, u + 1)
                dst = seq(m, 0, 128, 0, T)
                dve.tensor_tensor(dst, dst, p_b[:, 0:T], ALU.add).then_inc(x_ok, 1)

            def inverse_deviation(n, g, k):
                if g == 1 and live(n - 2):
                    m = n - 2
                    if k == 0:
                        dve.wait_ge(erv_ok, m + 1)
                        dve.tensor_tensor(nv[:], erv[:], erv[:], ALU.mult).then_inc(nv_ch, 1)
                    if k == 1:
                        dve.wait_ge(nv_ch, 3 * m + 1)
                        dve.scalar_tensor_tensor(nv[:], nv[:], -0.5, var[:], ALU.mult, ALU.mult).then_inc(nv_ch, 1)
                    if k == 2:
                        dve.wait_ge(nv_ch, 3 * m + 2)
                        dve.scalar_tensor_tensor(nv[:], nv[:], 1.5, erv[:], ALU.add, ALU.mult).then_inc(nv_ch, 1)
                    if k == 3:
                        dve.wait_ge(nv_ch, 3 * m + 3)
                        if live(n - 3):
                            dve.wait_ge(xn_ok, m)
                        dve.tensor_tensor(xh[:], xc[:], nv[:], ALU.mult).then_inc(xh_ok, 1)

            def centred(n, g):
                if g == 3 and live(n - 1):
                    m = n - 1
                    dve.wait_ge(mu_mm, m + 1)
                    dve.tensor_tensor(xc[:], xf[:], p_a[:, 0:T], ALU.subtract).then_inc(xc_ok, 1)

            def ffn_residual(n, g):
                if g == 0 and live(n - 3):
                    m = n - 3
                    dve.wait_ge(down_mm, m + 1)
                    dve.wait_ge(in_w2, 32 * loads(n, 3))
                    dst = seq(m, 0, 128, 0, T)
                    dve.scalar_tensor_tensor(dst, p_v[:, 0:T], b2[:], dst, ALU.add, ALU.add).then_inc(ffn_ok, 1)

            def unit(n, g):
                if has(n, g, 0):
                    rotate(n, g)
                else:
                    for k in range(4):
                        inverse_deviation(n, g, k)
                if g == 3 and live(n + 1):
                    dve.wait_ge(v_mm, 4 * n + 4)
                    shift_in(n + 1)
                if has(n, g, 2):
                    turned_probs(n, g)
                if has(n, g, 0):
                    norms(n, g)
                if has(n, g, 1):
                    softmax(n, g)
                ffn_residual(n, g)
                if has(n, g, 3):
                    residual(n, g)
                centred(n, g)
                if has(n, g, 1):
                    sums(n, g)

            schedule(dve, unit)
            dve.wait_ge(ffn_ok, NS)
            dve.tensor_tensor(x[:].rearrange("p (b t) -> p b t", b=B), x[:].rearrange("p (b t) -> p b t", b=B),
                              x1[:].rearrange("p (t b) -> p b t", b=B), ALU.add).then_inc(out_ok, 1)

        @block.gpsimd
        def _(pool):
            pool.wait_ge(in_c, 16 * 10)
            for l in range(LAYERS):
                for j in range(TILES):
                    ins = pool.tensor_tensor(tab[:, (l * TILES + j) * 256:(l * TILES + j + 1) * 256], rot[:, j].rearrange("p a b d -> p (a b d)"),
                                             scl[:, l].rearrange("p a b d -> p (a b d)"), ALU.mult)
            ins.then_inc(tab_ok, 1)

            def normalised(n, g):
                u = 4 * n + g
                for j in range(TILES):
                    pool.wait_ge(rot_ok, u * TILES + j + 1)
                    pool.tensor_tensor(cosp[:, j, :], cosp[:, j, :], sinp[:, j, :], ALU.add).then_inc(add_ok, 1)
                pool.wait_ge(rn_ok, u + 1)
                if has(n, g, 1):
                    pool.wait_ge(kT_mm, u)
                for j in range(TILES):
                    pool.wait_ge(add_ok, u * TILES + j + 1)
                    pool.tensor_tensor(qkn[:, j, :].rearrange("p (h d) -> p h d", d=HD),
                                       cosp[:, j, :].rearrange("p (h d) -> p h d", d=HD),
                                       rn[:, j, :].unsqueeze(2).broadcast_to([128, 2 * GH, HD]), ALU.mult).then_inc(qkn_ok, 1)

            def feed_forward(n, g):
                if g == 0 and live(n - 2):
                    m = n - 2
                    pool.wait_ge(xc_ok, m + 1)
                    if live(n - 3):
                        pool.wait_ge(var_mm, m)
                    pool.tensor_tensor(xq[:], xc[:], xc[:], ALU.mult).then_inc(xq_ok, 1)
                if g == 0 and live(n - 3):
                    m = n - 3
                    pool.wait_ge(gelu_ok, m + 1)
                    if live(n - 4):
                        pool.wait_ge(down_mm, m)
                    pool.tensor_tensor(fh[:], fa[:], fg[:], ALU.mult).then_inc(fh_ok, 1)

            def divide(n, g):
                u = 4 * n + g - 1
                pool.wait_ge(inv_ok, u + 1)
                p = prob[:].rearrange("p a j b c -> p (a j b) c")
                inv = pinv[:].rearrange("p a j b -> p (a j b)").unsqueeze(2).broadcast_to([128, 8, 2 * WIN])
                pool.tensor_tensor(p, p, inv, ALU.mult).then_inc(prob_ok, 1)

            def unit(n, g):
                feed_forward(n, g)
                if has(n, g, 0):
                    normalised(n, g)
                if has(n, g, 1):
                    divide(n, g)

            schedule(pool, unit)


def program(nc, io):
    with (nc.sbuf_tensor("hs", [128, TOK], F32) as hs, nc.sbuf_tensor("x1", [128, TOK], F32) as x1):
        with nc.sbuf_tensor("lstm_xw", [128, TOK * 4], F32) as lstm_xw:
            spiking_and_experts(nc, io, x1, lstm_xw)
            lstm(nc, io, hs, lstm_xw)
        transformer(nc, io, hs, x1)


def shape_constants():
    f = np.float32
    half = np.arange(0, HD, 2, dtype=f)
    inv_freq = f(1.0) / f(10000.0) ** (half / f(HD))
    t = np.arange(T, dtype=f)
    freqs = np.concatenate([t[:, None] * inv_freq[None, :]] * 2, -1)
    base = (half + f(0.4 * HD)) / f(1.4 * HD)
    power = (t - f(T // 2)) / f(WIN // 2)
    scale = np.concatenate([(base[None, :] ** power[:, None]).astype(f)] * 2, -1)
    cos, sin = np.cos(freqs).astype(f), np.sin(freqs).astype(f)
    sign = np.concatenate([-np.ones(32, f), np.ones(32, f)])
    inv = (f(1.0) / scale).astype(f)
    rot = np.zeros((T, 2, 2, HD), f)
    rot[:, 0, 0] = cos * scale * f(8.0 * RS)
    rot[:, 1, 0] = sign * sin * scale * f(8.0 * RS)
    rot[:, 0, 1] = cos * inv * f(RS)
    rot[:, 1, 1] = sign * sin * inv * f(RS)
    rot = rot.reshape(TILES, 128, 2, 2, HD).transpose(1, 0, 2, 3, 4)
    i = np.arange(128)[:, None]
    c = np.arange(2 * WIN)[None, :]
    ok = np.where(c < WIN, c >= i % WIN, c - WIN <= i % WIN)
    mask = np.zeros((128, TILES, 2, 2 * WIN), f)
    for j in range(TILES):
        first = (i < WIN) & (c < WIN) & (j == 0)
        mask[:, j] = np.where(ok & ~first, 0.0, -1e38)[:, None, :]
    return {
        "ident": np.eye(128, dtype=f), "off_diag": 1 - np.eye(128, dtype=f),
        "ones": np.full((128, 128), 1.0 / D, f),
        "mask": mask.reshape(128, -1), "rot": np.ascontiguousarray(rot),
        "iota": np.tile(np.arange(E, dtype=f), (128, 1)),
    }


def layouts(a):
    out = {}
    out["xT"] = a["x"].transpose(2, 1, 0).reshape(128, TOK)
    out["condT"] = a["cond_1024"].T
    out["wlif"] = a["L0_cond_W"].T
    out["vlif"] = a["L0_cond_V"]
    out["alpha_col"] = a["L0_cond_alpha"].reshape(128, 1)
    out["alpha_row"] = a["L0_cond_alpha"]
    out["wg"] = a["L0_ffn_Wg"]
    out["e_w1"] = a["L0_ffn_W1"].transpose(1, 0, 2).reshape(128, E * EH)
    out["e_b1"] = a["L0_ffn_b1"].reshape(E * HALVES, 128).T
    out["e_w2"] = a["L0_ffn_W2"].reshape(E * HALVES, 128, 128).transpose(1, 0, 2).reshape(128, -1)
    out["e_b2"] = a["L0_ffn_b2"]
    out["wx"] = a["L1_cond_Wx"]
    out["wh"] = a["L1_cond_Wh"]
    out["bx"] = a["L1_cond_b"].reshape(4, 128).T
    w = a["L1_ffn_Wqkv"].reshape(LAYERS, 128, 3, GROUPS, VC)
    out["wqkv"] = w.transpose(1, 0, 3, 2, 4).reshape(128, -1)
    out["q_scale"], out["k_scale"] = a["L1_ffn_q_scale"], a["L1_ffn_k_scale"]
    out["wo"] = a["L1_ffn_Wo"].reshape(LAYERS, 8, 128, 128).transpose(2, 0, 1, 3).reshape(128, -1)
    out["lnp"] = np.stack([a["L1_ffn_ln_g"], a["L1_ffn_ln_b"]], -1).transpose(1, 0, 2).reshape(128, -1)
    out["b2"] = a["L1_ffn_b2"].T
    w1 = np.zeros((LAYERS, 128, 2, FCH * FW), np.float32)
    w1[..., :FI] = a["L1_ffn_W1"].reshape(LAYERS, 128, 2, FI)
    out["w1"] = w1.transpose(1, 0, 2, 3).reshape(128, -1)
    b1 = np.zeros((LAYERS, 2, FCH * FW), np.float32)
    b1[..., :FI] = a["L1_ffn_b1"].reshape(LAYERS, 2, FI)
    b1p = np.zeros((128, LAYERS * 2 * FCH), np.float32)
    b1p[:FW] = b1.reshape(LAYERS * 2 * FCH, FW).T
    out["b1"] = b1p
    w2 = np.zeros((LAYERS, FCH * FW, 128), np.float32)
    w2[:, :FI] = a["L1_ffn_W2"]
    out["w2"] = w2.reshape(LAYERS, FCH, FW, 128).transpose(2, 0, 1, 3).reshape(FW, -1)
    out.update(shape_constants())
    return {k: np.ascontiguousarray(v) for k, v in out.items()}


def kernel(**inputs):
    import concourse.bacc as bacc
    from concourse.bass_utils import run_bass_kernel_spmd

    arrays = layouts({k: np.asarray(v) for k, v in inputs.items()})
    nc = bacc.Bacc("TRN2", target_bir_lowering=False, num_devices=1)
    io = {k: nc.dram_tensor(f"in_{k}", v.shape, mybir.dt.from_np(v.dtype), kind="ExternalInput").ap()
          for k, v in arrays.items()}
    io["out"] = nc.dram_tensor("out_x", (128, TOK), F32, kind="ExternalOutput").ap()
    program(nc, io)
    r = run_bass_kernel_spmd(nc, [{f"in_{k}": v for k, v in arrays.items()}], core_ids=[0])
    return r.results[0]["out_x"].reshape(128, B, T).transpose(1, 2, 0)
```
